# Optimizing a Trainium2 kernel written in Bass

```python
import numpy as np
import jax
import jax.numpy as jnp

def _softmax(x, axis=-1):
    return jax.nn.softmax(x, axis=axis)

def _gelu(x):
    return jax.nn.gelu(x, approximate=True)

def _silu(x):
    return jax.nn.silu(x)

def _sigmoid(x):
    return jax.nn.sigmoid(x)

def _layernorm(x, axis=-1, eps=1e-05):
    m = jnp.mean(x, axis=axis, keepdims=True)
    v = jnp.var(x, axis=axis, keepdims=True)
    return (x - m) / jnp.sqrt(v + eps)

def _scatter_add(tgt, idx, src, axis=0):
    return tgt.at[idx].add(src)

def _segment_sum(src, seg, n):
    return jax.ops.segment_sum(src, seg, n)
kernel_name = 'mk_adaln_d1_jaxref_r8_c0a7a7'

def setup_inputs(seed: int=0):
    np.random.seed(seed)
    _w = jnp.asarray

    def _L0_attn_setup():
        import jax, jax.numpy as jnp
        import numpy as np
        D_MODEL = 256
        NUM_HEADS = 16
        D_HEAD = D_MODEL // NUM_HEADS
        SCALE = 1.0 / np.sqrt(D_HEAD)
        key = jax.random.key(seed)
        ks = jax.random.split(key, 5)
        B, S = (4, 256)
        qkv = jax.random.normal(ks[0], (B, S, D_MODEL), dtype=jnp.float32)
        in_proj = jax.random.normal(ks[1], (3 * D_MODEL, D_MODEL), dtype=jnp.float32) * (1.0 / np.sqrt(D_MODEL))
        in_proj_bias = jnp.zeros((3 * D_MODEL,), dtype=jnp.float32)
        out_w = jax.random.normal(ks[2], (D_MODEL, D_MODEL), dtype=jnp.float32) * (1.0 / np.sqrt(D_MODEL))
        out_b = jnp.zeros((D_MODEL,), dtype=jnp.float32)
        alibi_slopes = (2.0 ** (-jnp.linspace(1.0, 8.0, NUM_HEADS))).astype(jnp.float32)
        return {'qkv': qkv, 'in_proj': in_proj, 'in_proj_bias': in_proj_bias, 'out_w': out_w, 'out_b': out_b, 'alibi_slopes': alibi_slopes}
    _L0_attn_in = _L0_attn_setup()

    def _L0_ffn_setup():
        import jax, jax.numpy as jnp
        import numpy as np
        TOP_K = 2
        LORA_SCALE = 32.0 / 16.0
        key = jax.random.key(seed)
        ks = jax.random.split(key, 11)
        B, S, D, F, E, R = (4, 128, 256, 704, 8, 16)
        sd, sf = (1.0 / np.sqrt(D), 1.0 / np.sqrt(F))
        return {'x': jax.random.normal(ks[0], (B, S, D), jnp.float32), 'gate_w': jax.random.normal(ks[1], (E, D), jnp.float32) * 0.02, 'w1': jax.random.normal(ks[2], (F, D), jnp.float32) * sd, 'w3': jax.random.normal(ks[3], (F, D), jnp.float32) * sd, 'w2': jax.random.normal(ks[4], (D, F), jnp.float32) * sf, 'a1': jax.random.normal(ks[5], (E, R, D), jnp.float32) * sd, 'b1': jax.random.normal(ks[6], (E, F, R), jnp.float32) * 0.01, 'a3': jax.random.normal(ks[7], (E, R, D), jnp.float32) * sd, 'b3': jax.random.normal(ks[8], (E, F, R), jnp.float32) * 0.01, 'a2': jax.random.normal(ks[9], (E, R, F), jnp.float32) * sf, 'b2': jax.random.normal(ks[10], (E, D, R), jnp.float32) * 0.01}
    _L0_ffn_in = _L0_ffn_setup()
    _L0_c = _w((lambda *s: np.random.randn(*s).astype(np.float32) * 0.05)(4, 256))
    _L0_wmod = _w((lambda *s: np.random.randn(*s).astype(np.float32) * 0.05)(256, 6 * 256) * 256 ** (-0.5))
    _d = {'L0_attn_qkv': _L0_attn_in['qkv'], 'L0_attn_in_proj': _L0_attn_in['in_proj'], 'L0_attn_in_proj_bias': _L0_attn_in['in_proj_bias'], 'L0_attn_out_w': _L0_attn_in['out_w'], 'L0_attn_out_b': _L0_attn_in['out_b'], 'L0_attn_alibi_slopes': _L0_attn_in['alibi_slopes'], 'L0_ffn_gate_w': _L0_ffn_in['gate_w'], 'L0_ffn_w1': _L0_ffn_in['w1'], 'L0_ffn_w3': _L0_ffn_in['w3'], 'L0_ffn_w2': _L0_ffn_in['w2'], 'L0_ffn_a1': _L0_ffn_in['a1'], 'L0_ffn_b1': _L0_ffn_in['b1'], 'L0_ffn_a3': _L0_ffn_in['a3'], 'L0_ffn_b3': _L0_ffn_in['b3'], 'L0_ffn_a2': _L0_ffn_in['a2'], 'L0_ffn_b2': _L0_ffn_in['b2'], 'L0_c': _L0_c, 'L0_wmod': _L0_wmod}
    _x0 = _d['L0_attn_qkv']
    _d['L0_attn_qkv'] = jax.random.normal(jax.random.fold_in(jax.random.key(seed), 1), (4, 512, 256), dtype=_x0.dtype)
    del _x0
    return _d

def reference(L0_attn_qkv, L0_attn_in_proj, L0_attn_in_proj_bias, L0_attn_out_w, L0_attn_out_b, L0_attn_alibi_slopes, L0_ffn_gate_w, L0_ffn_w1, L0_ffn_w3, L0_ffn_w2, L0_ffn_a1, L0_ffn_b1, L0_ffn_a3, L0_ffn_b3, L0_ffn_a2, L0_ffn_b2, L0_c, L0_wmod):

    def _L0_attn_ref(qkv, in_proj, in_proj_bias, out_w, out_b, alibi_slopes):
        import jax, jax.numpy as jnp
        import numpy as np
        D_MODEL = 256
        NUM_HEADS = 16
        D_HEAD = D_MODEL // NUM_HEADS
        SCALE = 1.0 / np.sqrt(D_HEAD)
        B, S, D = qkv.shape
        H, Dh = (NUM_HEADS, D_HEAD)
        proj = qkv @ in_proj.T + in_proj_bias
        q, k, v = jnp.split(proj, 3, axis=-1)
        q = q.reshape(B, S, H, Dh).transpose(0, 2, 1, 3)
        k = k.reshape(B, S, H, Dh).transpose(0, 2, 1, 3)
        v = v.reshape(B, S, H, Dh).transpose(0, 2, 1, 3)
        scores = jnp.einsum('bhqd,bhkd->bhqk', q, k) * SCALE
        pos = jnp.arange(S)
        rel = (pos[None, :] - pos[:, None]).astype(scores.dtype)
        scores = scores + rel[None, None] * alibi_slopes[None, :, None, None]
        causal_mask = pos[None, :] > pos[:, None]
        scores = jnp.where(causal_mask[None, None], -jnp.inf, scores)
        attn = jnp.maximum(jax.nn.softmax(scores, axis=-1), 1e-10)
        attended = jnp.einsum('bhqk,bhkd->bhqd', attn, v)
        attended = attended.transpose(0, 2, 1, 3).reshape(B, S, D)
        return attended @ out_w.T + out_b

    def _L0_ffn_ref(x, gate_w, w1, w3, w2, a1, b1, a3, b3, a2, b2):
        import jax, jax.numpy as jnp
        import numpy as np
        TOP_K = 2
        LORA_SCALE = 32.0 / 16.0
        B, S, D = x.shape
        E = gate_w.shape[0]
        xf = x.reshape(B * S, D)
        N = xf.shape[0]
        logits = xf @ gate_w.T
        top_w, top_i = jax.lax.top_k(logits, TOP_K)
        routing = jax.nn.softmax(top_w, axis=-1)
        w_full = jnp.zeros((N, E), x.dtype).at[jnp.arange(N)[:, None], top_i].add(routing)
        base1 = xf @ w1.T
        base3 = xf @ w3.T

        def expert_step(acc, p):
            A1, B1, A3, B3, A2, B2, we = p
            h1 = base1 + xf @ A1.T @ B1.T * LORA_SCALE
            h3 = base3 + xf @ A3.T @ B3.T * LORA_SCALE
            act = jax.nn.silu(h1) * h3
            out = act @ w2.T + act @ A2.T @ B2.T * LORA_SCALE
            return (acc + we[:, None] * out, None)
        init = jnp.zeros((N, D), x.dtype)
        out, _ = jax.lax.scan(expert_step, init, (a1, b1, a3, b3, a2, b2, w_full.T))
        return out.reshape(B, S, D)
    x = L0_attn_qkv
    mod = (_silu(L0_c) @ L0_wmod).reshape(L0_c.shape[0], 6, 1, -1)
    sa, ca, ga, sb, cb, gb = (mod[:, 0], mod[:, 1], mod[:, 2], mod[:, 3], mod[:, 4], mod[:, 5])
    ga = (2 * (ga >= 0) - 1) * jnp.maximum(jnp.abs(ga), 0.25)
    gb = (2 * (gb >= 0) - 1) * jnp.maximum(jnp.abs(gb), 0.25)
    h = _layernorm(x, axis=-1) * (1 + ca) + sa
    x = x + ga * _L0_attn_ref(h, L0_attn_in_proj, L0_attn_in_proj_bias, L0_attn_out_w, L0_attn_out_b, L0_attn_alibi_slopes)
    h = _layernorm(x, axis=-1) * (1 + cb) + sb
    x = x + gb * _L0_ffn_ref(h, L0_ffn_gate_w, L0_ffn_w1, L0_ffn_w3, L0_ffn_w2, L0_ffn_a1, L0_ffn_b1, L0_ffn_a3, L0_ffn_b3, L0_ffn_a2, L0_ffn_b2)
    return x

_drawn_inputs = setup_inputs


def setup_inputs(seed=0):
    import zlib

    import numpy as np

    out = dict(_drawn_inputs(seed))
    spreads = {'L0_attn_in_proj_bias': (0.0, 0.283), 'L0_attn_out_b': (0.0, 0.337)}
    factors = {'L0_ffn_gate_w': 4.463,
     'L0_ffn_a1': 6.533,
     'L0_ffn_b1': 6.526,
     'L0_ffn_a3': 6.76,
     'L0_ffn_b3': 6.805,
     'L0_ffn_a2': 6.756,
     'L0_ffn_b2': 6.784}
    for name, (base, spread) in spreads.items():
        noise = np.random.default_rng([zlib.crc32(name.encode()), seed]).standard_normal(out[name].shape)
        drawn = base * np.exp(spread * noise) if base else spread * noise
        out[name] = jnp.asarray(drawn.astype(out[name].dtype))
    for name, factor in factors.items():
        out[name] = (out[name] * factor).astype(out[name].dtype)
    return out
```

```python
from contextlib import ExitStack

import concourse.bass as bass
from concourse import mybir

P = 128
ALU = mybir.AluOpType
ACT = mybir.ActivationFunctionType
BF16 = mybir.dt.bfloat16
F32 = mybir.dt.float32
U32 = mybir.dt.uint32

LN_EPS = 1e-5
GATE_FLOOR = 0.25
PROB_FLOOR = 1e-10
LORA_SCALE = 2.0
MASKED = -3e38


def adaln_block(nc, x, wqkvT, bqk, bv, woT, bo, slopes, gateT, w13T, w2T, a13T, b13T, a2T, b2T, cT, wmod,
                consts, pos_rows, out):
    B, S, D = x.shape
    H = slopes.shape[0]
    DH = D // H
    F = w2T.shape[0]
    E = gateT.shape[1]
    KT = D // P
    NB = S // P
    G = 4
    NG = H // G
    NF = F // P
    FT = F - NF * P
    NFT = NF + 1
    NQK = 2 * KT
    SCALE = float(DH) ** -0.5
    assert (B, S, D, H, F, E) == (4, 512, 256, 16, 704, 8) and FT == 64 and b13T.shape[0] == P

    R_SLOPE = 6 * DH
    R_POS = R_SLOPE + 3
    R_NORM = R_SLOPE + 6
    R_ALL = R_SLOPE + 9
    Q_PART = (0, 0, 1, 0, 1, 2)
    K_PART = (0, 1, 0, 2, 1, 0)

    COLS = 1280
    START1, WIDTH1 = (896, 1024, 512, 0), (128, 256, 384, 512)
    START2, WIDTH2 = (0, 512, 1024, 896), (512, 384, 256, 128)

    tasks = [("p1", h) for h in range(8)]
    for h in range(8):
        tasks += [("p2", h), ("p1", 8 + h)]
    tasks += [("p2", h) for h in range(8, H)]
    later = {}
    for n, (kind, h) in enumerate(tasks):
        if kind == "p1" and h % G == G - 1:
            later.setdefault(n + 1, []).append(("norm", h // G))
            later.setdefault(n + 2, []).append(("norm_t", h // G))
        if kind == "p2" and h % G == G - 1:
            later.setdefault(n + 1, []).append(("pv", h // G))
    steps = []
    for n in range(len(tasks) + 2):
        if n < len(tasks):
            steps.append((*tasks[n], n))
        steps += [(kind, g, n) for kind, g in later.get(n, [])]

    with ExitStack() as ctx:
        def sb(name, shape, dt=F32):
            return ctx.enter_context(nc.sbuf_tensor(name, shape, dt))

        ps = ctx.enter_context(nc.psum_tensor("ps", [P, 8, 512], F32))
        psb = ps[:].rearrange("p k n -> p (k n)")
        scratch = nc.dram_tensor("qk_scratch", (NQK * P, 3, S), BF16, kind="Internal").ap()

        const = sb("const", [P, 896])
        ident, qmask, kmask, ecol = const[:, 0:128], const[:, 128:640], const[:, 640:768], const[:, 768:896]
        ident_b, kmask_b = sb("ident_b", [P, P], BF16), sb("kmask_b", [P, P], BF16)
        floor_c = sb("floor_c", [P, P])
        wqkv = sb("wqkv", [P, KT, 3 * D])
        wo = sb("wo", [P, NG, D])
        w13 = sb("w13", [P, KT, 2 * F])
        b13 = sb("b13", [P, 2 * F])
        a13 = sb("a13", [P, KT, 2 * P])
        w2, a2, b2 = sb("w2", [P, NFT, D]), sb("a2", [P, NFT, P]), sb("b2", [P, D])
        gate_w = sb("gate_w", [P, KT, E])
        b_qk, b_v, b_o = sb("b_qk", [P, NQK]), sb("b_v", [P, D]), sb("b_o", [P, D])
        c_t, c_silu = sb("c_t", [P, KT, B]), sb("c_silu", [P, KT, B])
        mod_t = sb("mod_t", [P, 4, KT, B])
        gates = sb("gates", [P, B, 2, D])
        slope, slope_r = sb("slope", [H, 1]), sb("slope_r", [H, 2])
        slope_p = sb("slope_p", [H, 3], BF16)
        slope_w = sb("slope_w", [H, 6, S], BF16)

        xs = sb("xs", [P, B * NB, D])
        stats, mv = sb("stats", [P, NB, 6]), sb("mv", [P, NB, 2])
        veps, lnv, rstd = sb("veps", [P, NB]), sb("lnv", [P, NB]), sb("rstd", [P, NB])
        xhat = sb("xhat", [P, NB, D])
        modc = sb("modc", [P, 2, 2, KT])
        hT, h2T = sb("hT", [P, KT, S]), sb("h2T", [P, KT, S])
        qk_f, qk_r = sb("qk_f", [P, 2, S]), sb("qk_r", [P, S])
        qk_p = sb("qk_p", [P, NQK, 3, S], BF16)
        QA, KA = sb("QA", [P, H, S], BF16), sb("KA", [P, H, S], BF16)
        V, Vsuf = sb("V", [P, NB, H, 32]), sb("Vsuf", [P, 2, H, 32])
        shift, zsum = sb("shift", [P, H, NB]), sb("zsum", [P, H, NB])
        lnz, lse, lse_r = sb("lnz", [P, G * NB]), sb("lse", [P, G * NB]), sb("lse_r", [P, G * NB])
        lse_p, lse_t = sb("lse_p", [P, 3, G * NB], BF16), sb("lse_t", [3 * G * NB, P], BF16)
        NPROB = 6
        prob = sb("prob", [P, NPROB, COLS])
        att = sb("att", [P, NG, S])
        ysb, osb = sb("ysb", [P, D]), sb("osb", [P, D])
        early = prob[:].rearrange("p g n -> p (g n)")
        wmod_s = early[:, 0:KT * 6 * D].rearrange("p (k n) -> p k n", k=KT)
        c_wide = early[:, 3072:3072 + KT * B * P].rearrange("p (k b n) -> p k b n", k=KT, b=B)
        g_abs, g_sgn = early[:, 4096:4608], early[:, 4608:5120]

        logit, top, top_i = sb("logit", [P, NB, E]), sb("top", [P, NB, 8]), sb("top_i", [P, NB, 8], U32)
        top_f = sb("top_f", [P, NB, 2])
        rdiff, rexp, rsum, rw = sb("rdiff", [P, NB]), sb("rexp", [P, NB]), sb("rsum", [P, NB]), sb("rw", [P, NB])
        pick = sb("pick", [P, 3, NB, P])
        pickT = early[:, 0:4 * S].rearrange("p (k n) -> p k n", k=4)
        pickw = early[:, 4 * S:7 * S].rearrange("p (k n) -> p k n", k=3)
        um = early[:, 7 * S:11 * S].rearrange("p (k n) -> p k n", k=4)
        sil = early[:, 11 * S:13 * S].rearrange("p (k n) -> p k n", k=2)
        gw = early[:, 13 * S:15 * S].rearrange("p (k n) -> p k n", k=2)
        act1, act2 = hT, sb("act2", [P, 2, S])
        gsum = sb("gsum", [P, 2, S])
        tm = gw

        per = dict(
            ln1_stat=NB, ln1_aggr=NB, ln1_veps=1, ln1_lnv=1, ln1_rstd=1, ln1_xhat=NB, h1T_ps=KT, h1T_ready=KT,
            ln2_stat=NB, ln2_aggr=NB, ln2_veps=1, ln2_lnv=1, ln2_rstd=1, ln2_xhat=NB, h2T_ps=KT, h2T_ready=KT,
            mod1_now=1, mod2_now=1, qk_ps=NQK, qk_evac=NQK, qk_hi=NQK, qk_res=NQK, qk_mid=NQK, qk_parts=NQK, v_ps=NB, v_ready=NB,
            vsuf_mid=1, vsuf_ready=1, q_out=16, k_out=16, rows_landed=16 * 12,
            p1_ps=H, p1_max=H, p1_done=H, lnz_ready=NG, lse_ready=NG, lse_hi=NG, lse_res=NG, lse_mid=NG, lse_parts=NG,
            lse_ps=NG, lse_evac=NG, lse_landed=48 * NG, p2_ps=H, p2_exp=H, p2_ready=H, pv_ps=NG, att_ready=NG,
            y_ps=NB, y_biased=NB, y_gated=NB, x1_ready=NB,
            logit_ps=1, logit_ready=1, top_ready=NB, topi_ready=NB, topf_ready=1, rdiff_ready=1, rexp_ready=1,
            rsum_ready=1, rw_ready=1, pick_ready=3, pick_ps=3, pickT_ready=4, pickd_ready=1, pickw_ready=2, u_ps=2, um_ready=4,
            fa_ps=NFT, fa_sil=NFT, fa_act=NFT, fb_ps=NFT, fb_sil=NFT, fb_act=NFT, gw_ready=2 * NFT, gsum_ready=NFT,
            down_ps=NFT, tm_1=1, tm_2=1, tm_ready=1, o_ps=NB, o_gated=NB, o_ready=NB, store_done=16 * NB)
        once = """const_in x_in c_in wmod_in wqkv_in small_in rows_in out_w_in zero_done ffn_in cs_ready cwide_ready
            mod_ps mod_evac modt_ready gate_ps gate_abs gate_sgn gate_neg gate_floor gates_ready sl_1 sl_2 sl_3 sl_4 sl_5
            slope_wide bq_scaled const_ready""".split()
        s = {n: ctx.enter_context(nc.semaphore(n)) for n in [*per, *once]}
        block = ctx.enter_context(nc.Block())

        def wait(eng, name, b, k):
            eng.wait_ge(s[name], b * per[name] + k)

        def wait_apart(eng, name, b, k):
            value = b * per[name] + k
            if not isinstance(b, int):
                value = eng.to_reg(value)
            eng.wait_ge(s["const_ready"], 2)
            eng.wait_ge(s[name], value)

        def tile_cols(f):
            return (f * 2 * P, P) if f < NF else (NF * 2 * P, FT)

        @block.sync
        def _(sp):
            def load(dst, src, name):
                sp.dma_start(dst, src).then_inc(s[name], 16)

            xv = x.rearrange("b (i p) d -> p (b i) d", p=P)
            load(xs[:, 0:NB, :], xv[:, 0:NB, :], "x_in")
            load(c_t[:], cT.rearrange("(k p) b -> p k b", p=P), "c_in")
            load(const[:], consts, "const_in")
            load(wqkv[:], wqkvT.rearrange("(k p) n -> p k n", p=P), "wqkv_in")
            load(b_qk[:], bqk, "small_in")
            load(b_v[:], bv.rearrange("(o d) -> o d", o=1).to_broadcast([P, D]), "small_in")
            load(b_o[:], bo.rearrange("(o d) -> o d", o=1).to_broadcast([P, D]), "small_in")
            load(slope[:], slopes.rearrange("(h o) -> h o", o=1), "small_in")
            load(gate_w[:], gateT.rearrange("(k p) e -> p k e", p=P), "small_in")
            for i in range(3):
                load(QA[R_POS + i:R_POS + i + 1, :, :], pos_rows[0], "rows_in")
                load(KA[R_SLOPE + i:R_SLOPE + i + 1, :, :], pos_rows[0], "rows_in")
                load(KA[R_NORM + i:R_NORM + i + 1, :, :], pos_rows[1], "rows_in")
            load(xs[:, NB:, :], xv[:, NB:, :], "x_in")
            sp.wait_ge(s["slope_wide"], 6)
            for i in range(3):
                load(QA[R_SLOPE + i:R_SLOPE + i + 1, :, :], slope_w[:, i, :], "rows_in")
                load(KA[R_POS + i:R_POS + i + 1, :, :], slope_w[:, 3 + i, :], "rows_in")

            def regroup(b):
                for side, name in ((0, "q_out"), (1, "k_out")):
                    wait(sp, "qk_parts", b, (side + 1) * KT)
                    sp.dma_start(scratch[side * D:(side + 1) * D].rearrange("(t p) c q -> p t c q", p=P),
                                 qk_p[:, side * KT:(side + 1) * KT, :, :]).then_inc(s[name], 16)
                for side, name, dst, parts in ((0, "q_out", QA, Q_PART), (1, "k_out", KA, K_PART)):
                    wait(sp, name, b, 16)
                    src = scratch[side * D:(side + 1) * D].rearrange("(h d) c q -> d h c q", d=DH)
                    for r, part in enumerate(parts):
                        sp.dma_start(dst[r * DH:(r + 1) * DH, :, :], src[:, :, part, :]).then_inc(s["rows_landed"], 16)

            def attention(b):
                for g in range(NG):
                    wait(sp, "lse_evac", b, g + 1)
                    for i in range(3):
                        sp.dma_start(QA[R_NORM + i:R_NORM + i + 1, g * G:(g + 1) * G, :],
                                     lse_t[i * G * NB:(i + 1) * G * NB, :]).then_inc(s["lse_landed"], 16)

            def ffn(b):
                for i in range(NB):
                    wait(sp, "o_ready", b, i + 1)
                    sp.dma_start(out[b, i * P:(i + 1) * P, :], xs[:, b * NB + i, :]).then_inc(s["store_done"], 16)

            regroup(0)
            with sp.Fori(0, B - 1) as b:
                attention(b)
                regroup(b + 1)
                ffn(b)
            attention(B - 1)
            ffn(B - 1)
            sp.wait_ge(s["store_done"], B * per["store_done"])

        @block.gpsimd
        def _(pool):
            def load(dst, src, name):
                pool.dma_start(dst, src).then_inc(s[name], 16)

            load(wmod_s, wmod.rearrange("(k p) n -> p k n", p=P), "wmod_in")
            nc.gpsimd.memset(V[:], 0.0).then_inc(s["zero_done"], 1)
            nc.gpsimd.memset(wo[:], 0.0).then_inc(s["zero_done"], 1)
            nc.gpsimd.memset(w2[:], 0.0).then_inc(s["zero_done"], 1)
            nc.gpsimd.memset(a2[:], 0.0).then_inc(s["zero_done"], 1)
            nc.gpsimd.memset(floor_c[:], PROB_FLOOR).then_inc(s["zero_done"], 1)
            pool.wait_ge(s["zero_done"], 4)
            wov = woT.rearrange("(g c d) n -> c d g n", c=G, d=DH)
            for c in range(G):
                load(wo[32 * c:32 * c + DH, :, :], wov[c], "out_w_in")
            load(w13[:], w13T.rearrange("(k p) n -> p k n", p=P), "ffn_in")
            load(b13[:], b13T, "ffn_in")
            load(a13[:], a13T.rearrange("(k p) n -> p k n", p=P), "ffn_in")
            load(w2[:, 0:NF, :], w2T[0:NF * P].rearrange("(f p) n -> p f n", p=P), "ffn_in")
            load(w2[0:FT, NF, :], w2T[NF * P:F], "ffn_in")
            load(a2[:, 0:NF, :], a2T[0:NF * P].rearrange("(f p) n -> p f n", p=P), "ffn_in")
            load(a2[0:FT, NF, :], a2T[NF * P:F], "ffn_in")
            load(b2[:], b2T, "ffn_in")

            def front(b):
                wait(pool, "v_ready", b, NB)
                nc.gpsimd.tensor_tensor(Vsuf[:, 1], V[:, 2], V[:, 3], ALU.add).then_inc(s["vsuf_mid"], 1)
                wait(pool, "vsuf_mid", b, 1)
                nc.gpsimd.tensor_tensor(Vsuf[:, 0], V[:, 1], Vsuf[:, 1], ALU.add).then_inc(s["vsuf_ready"], 1)

            def ffn(b):
                wait(pool, "pickT_ready", b, 2)
                nc.gpsimd.tensor_tensor(pickw[:, 2, :], pickT[:, 1, :], pickT[:, 0, :], ALU.subtract).then_inc(s["pickd_ready"], 1)
                wait(pool, "pickT_ready", b, 4)
                for k in range(2):
                    nc.gpsimd.tensor_tensor(pickw[:, k, :], pickT[:, k, :], pickT[:, 2 + k, :], ALU.mult).then_inc(s["pickw_ready"], 1)
                for f in range(NFT):
                    m = P if f < NF else FT
                    wait(pool, "fa_act", b, f + 1)
                    if f >= 1:
                        wait(pool, "gsum_ready", b, f)
                    nc.gpsimd.tensor_tensor(gw[0:m, 0, :], act1[0:m, f % 2, :], pickT[0:m, 2, :], ALU.mult).then_inc(s["gw_ready"], 1)
                    wait(pool, "fb_act", b, f + 1)
                    nc.gpsimd.tensor_tensor(gw[0:m, 1, :], act2[0:m, f % 2, :], pickT[0:m, 3, :], ALU.mult).then_inc(s["gw_ready"], 1)

            front(0)
            with pool.Fori(0, B - 1) as b:
                front(b + 1)
                ffn(b)
            ffn(B - 1)

        @block.scalar
        def _(act):
            def layer_norm(b, n):
                wait(act, f"ln{n}_veps", b, 1)
                nc.scalar.activation(lnv[:], veps[:], ACT.Ln).then_inc(s[f"ln{n}_lnv"], 1)
                wait(act, f"ln{n}_lnv", b, 1)
                nc.scalar.activation(rstd[:], lnv[:], ACT.Exp, scale=-0.5).then_inc(s[f"ln{n}_rstd"], 1)

            def modulate(b, n, dst, bank):
                wait(act, f"mod{n}_now", b, 1)
                for k in range(KT):
                    wait(act, f"h{n}T_ps", b, k + 1)
                    nc.scalar.activation(dst[:, k, :], ps[:, bank + k, :], ACT.Identity, scale=modc[:, n - 1, 1, k:k + 1],
                                         bias=modc[:, n - 1, 0, k:k + 1]).then_inc(s[f"h{n}T_ready"], 1)

            def front(b):
                layer_norm(b, 1)
                modulate(b, 1, hT, 4)
                for t in range(NQK):
                    wait(act, "qk_ps", b, t + 1)
                    if t >= 2:
                        wait(act, "qk_res", b, t - 1)
                    nc.scalar.activation(qk_f[:, t % 2, :], ps[:, t, :], ACT.Identity, bias=b_qk[:, t:t + 1],
                                         scale=SCALE if t < KT else 1.0).then_inc(s["qk_evac"], 1)

            def attention(b):
                for kind, h, n in steps:
                    base = (n % 2) * 1536
                    if kind == "p1":
                        wait(act, "p1_max", b, h + 1)
                        for i in range(NB):
                            a = base + START1[i]
                            last = nc.scalar.activation(psb[:, a:a + WIDTH1[i]], psb[:, a:a + WIDTH1[i]], ACT.Exp, scale=-1.0,
                                                        bias=shift[:, h, i:i + 1], accum_out=zsum[:, h, i:i + 1])
                        last.then_inc(s["p1_done"], 1)
                    elif kind == "norm":
                        wait(act, "p1_done", b, G * (h + 1))
                        nc.scalar.activation(lnz[:], zsum[:, G * h:G * (h + 1), :].rearrange("p h i -> p (h i)"),
                                             ACT.Ln).then_inc(s["lnz_ready"], 1)
                    elif kind == "norm_t":
                        wait(act, "lse_ps", b, h + 1)
                        if h >= 1:
                            wait(act, "lse_landed", b, 48 * h)
                        nc.scalar.copy(lse_t[:], ps[:, 7, :].bitcast(BF16)[0:3 * G * NB, 0:P]).then_inc(s["lse_evac"], 1)
                    elif kind == "p2":
                        wait(act, "p2_ps", b, h + 1)
                        if h >= NPROB:
                            wait(act, "pv_ps", b, (h - NPROB) // G + 1)
                        nc.scalar.activation(prob[:, h % NPROB, :], psb[:, base:base + COLS], ACT.Exp).then_inc(s["p2_exp"], 1)
                    elif kind == "pv":
                        wait(act, "pv_ps", b, h + 1)
                        nc.scalar.copy(att[:, h, :], ps[:, 6, :]).then_inc(s["att_ready"], 1)

            def ffn(b):
                layer_norm(b, 2)
                modulate(b, 2, h2T, 6)
                wait(act, "rdiff_ready", b, 1)
                nc.scalar.activation(rexp[:], rdiff[:], ACT.Exp).then_inc(s["rexp_ready"], 1)
                for k, bank in ((0, 6), (1, 7), (2, 5)):
                    wait(act, "pick_ps", b, k + 1)
                    nc.scalar.copy(pickT[:, k, :], ps[:, bank, :]).then_inc(s["pickT_ready"], 1)
                nc.scalar.activation(pickT[:, 3, :], ps[:, 5, :], ACT.Identity, scale=-1.0, bias=1.0).then_inc(s["pickT_ready"], 1)

                def silu(f, name_ps, name_out, ones_before):
                    wait(act, name_ps, b, f + 1)
                    for name, k in ones_before:
                        wait(act, name, b, k)
                    if f < NF:
                        nc.scalar.activation(sil[:, ones_before_slot(name_out), :], ps[:, 2 * (f % 2), :], ACT.Silu).then_inc(s[name_out], 1)
                    else:
                        nc.scalar.activation(sil[FT:2 * FT, ones_before_slot(name_out), :], ps[0:FT, 2 * (f % 2), :],
                                             ACT.Silu).then_inc(s[name_out], 1)

                def ones_before_slot(name):
                    return 0 if name == "fa_sil" else 1

                for f in range(NFT + 1):
                    if f < NFT:
                        silu(f, "fa_ps", "fa_sil", [("fa_act", f)] if f else [])
                    if f >= 1:
                        silu(f - 1, "fb_ps", "fb_sil", [("fb_act", f - 1)] if f >= 2 else [])

            act.wait_ge(s["c_in"], 16)
            nc.scalar.activation(c_silu[:], c_t[:], ACT.Silu).then_inc(s["cs_ready"], 1)
            front(0)
            with act.Fori(0, B - 1) as b:
                attention(b)
                front(b + 1)
                ffn(b)
            attention(B - 1)
            ffn(B - 1)

        @block.vector
        def _(dve):
            def layer_norm(b, n):
                for i in range(NB):
                    nc.vector.bn_stats(stats[:, i, :], xs[:, b * NB + i, :]).then_inc(s[f"ln{n}_stat"], 1)
                for i in range(NB):
                    wait_apart(dve, f"ln{n}_stat", b, i + 1)
                    nc.vector.bn_aggr(mv[:, i, :], stats[:, i, :]).then_inc(s[f"ln{n}_aggr"], 1)
                wait(dve, f"ln{n}_aggr", b, NB)
                nc.vector.tensor_scalar(veps[:], mv[:, :, 1], LN_EPS, None, ALU.add).then_inc(s[f"ln{n}_veps"], 1)
                wait(dve, f"ln{n}_rstd", b, 1)
                for i in range(NB):
                    nc.vector.tensor_scalar(xhat[:, i, :], xs[:, b * NB + i, :], mv[:, i, 0:1], rstd[:, i:i + 1],
                                            ALU.subtract, ALU.mult).then_inc(s[f"ln{n}_xhat"], 1)

            def mod_of(b, n):
                nc.vector.tensor_copy(modc[:, n - 1].rearrange("p a k -> p (a k)"),
                                      mod_t[:, 2 * n - 2:2 * n].rearrange("p a k b -> p (a k) b")[:, :, b]).then_inc(s[f"mod{n}_now"], 1)

            def front(b, first=False):
                layer_norm(b, 1)
                if first:
                    modulation()
                mod_of(b, 1)
                for t in range(NQK):
                    wait(dve, "qk_evac", b, t + 1)
                    nc.vector.tensor_copy(qk_p[:, t, 0, :], qk_f[:, t % 2, :]).then_inc(s["qk_hi"], 1)
                    wait(dve, "qk_hi", b, t + 1)
                    nc.vector.tensor_tensor(qk_r[:], qk_f[:, t % 2, :], qk_p[:, t, 0, :], ALU.subtract).then_inc(s["qk_res"], 1)
                    wait(dve, "qk_res", b, t + 1)
                    nc.vector.tensor_copy(qk_p[:, t, 1, :], qk_r[:]).then_inc(s["qk_mid"], 1)
                    wait(dve, "qk_mid", b, t + 1)
                    nc.vector.tensor_tensor(qk_p[:, t, 2, :], qk_r[:], qk_p[:, t, 1, :], ALU.subtract).then_inc(s["qk_parts"], 1)
                for i in range(NB):
                    wait(dve, "v_ps", b, i // 2 * 2 + 2)
                    nc.vector.tensor_tensor(V[:, i, :, 0:DH], ps[:, 4 + i // 2, (i % 2) * D:(i % 2 + 1) * D].rearrange("p (h d) -> p h d", h=H),
                                            b_v[:].rearrange("p (h d) -> p h d", h=H), ALU.add).then_inc(s["v_ready"], 1)

            def modulation():
                dve.wait_ge(s["cs_ready"], 1)
                nc.vector.tensor_copy(c_wide, c_silu[:].rearrange("p k (b o) -> p k b o", o=1).to_broadcast([P, KT, B, P])).then_inc(s["cwide_ready"], 1)
                dve.wait_ge(s["mod_ps"], 1)
                mods = ps[:, 0, 0:4 * KT * B].rearrange("p (a k b) -> p a k b", a=4, k=KT)
                for a in range(4):
                    nc.vector.tensor_scalar(mod_t[:, a], mods[:, a], float(a % 2), None, ALU.add).then_inc(s["modt_ready"], 1)
                dve.wait_ge(s["modt_ready"], 4)

            def attention(b):
                for kind, h, n in steps:
                    base = (n % 2) * 1536
                    if kind == "p1":
                        wait_apart(dve, "p1_ps", b, h + 1)
                        for i in range(NB):
                            a = base + START1[i]
                            last = nc.vector.tensor_tensor_reduce(out=psb[:, a:a + WIDTH1[i]], in0=psb[:, a:a + WIDTH1[i]],
                                                                  in1=qmask[:, S - WIDTH1[i]:S], scale=-1.0, scalar=3.3e38, op0=ALU.add,
                                                                  op1=ALU.min, accum_out=shift[:, h, i:i + 1])
                        last.then_inc(s["p1_max"], 1)
                    elif kind == "norm":
                        wait(dve, "lnz_ready", b, h + 1)
                        nc.vector.tensor_tensor(lse[:], shift[:, G * h:G * (h + 1), :].rearrange("p h i -> p (h i)"), lnz[:],
                                                ALU.subtract).then_inc(s["lse_ready"], 1)
                        wait(dve, "lse_ready", b, h + 1)
                        nc.vector.tensor_copy(lse_p[:, 0, :], lse[:]).then_inc(s["lse_hi"], 1)
                        wait(dve, "lse_hi", b, h + 1)
                        nc.vector.tensor_tensor(lse_r[:], lse[:], lse_p[:, 0, :], ALU.subtract).then_inc(s["lse_res"], 1)
                        wait(dve, "lse_res", b, h + 1)
                        nc.vector.tensor_copy(lse_p[:, 1, :], lse_r[:]).then_inc(s["lse_mid"], 1)
                        wait(dve, "lse_mid", b, h + 1)
                        nc.vector.tensor_tensor(lse_p[:, 2, :], lse_r[:], lse_p[:, 1, :], ALU.subtract).then_inc(s["lse_parts"], 1)
                    elif kind == "p2":
                        wait(dve, "p2_exp", b, h + 1)
                        nc.vector.tensor_scalar(prob[:, h % NPROB, :], prob[:, h % NPROB, :], PROB_FLOOR, None, ALU.max).then_inc(s["p2_ready"], 1)
                for i in range(NB):
                    wait(dve, "y_ps", b, i // 2 * 2 + 2)
                    if i >= 1:
                        wait(dve, "x1_ready", b, i)
                    nc.vector.tensor_tensor(ysb[:], ps[:, 6 + i // 2, (i % 2) * D:(i % 2 + 1) * D], b_o[:], ALU.add).then_inc(s["y_biased"], 1)
                    wait(dve, "y_biased", b, i + 1)
                    nc.vector.tensor_tensor(ysb[:], ysb[:], gates[:, b, 0, :], ALU.mult).then_inc(s["y_gated"], 1)
                    wait(dve, "y_gated", b, i + 1)
                    nc.vector.tensor_tensor(xs[:, b * NB + i, :], xs[:, b * NB + i, :], ysb[:], ALU.add).then_inc(s["x1_ready"], 1)

            def ffn(b):
                wait_apart(dve, "x1_ready", b, NB)
                layer_norm(b, 2)
                mod_of(b, 2)
                wait(dve, "logit_ps", b, 1)
                nc.vector.tensor_copy(logit[:].rearrange("p i e -> p (i e)"), ps[:, 4, 0:NB * E]).then_inc(s["logit_ready"], 1)
                wait_apart(dve, "logit_ready", b, 1)
                for i in range(NB):
                    nc.vector.max(top[:, i, :], logit[:, i, :]).then_inc(s["top_ready"], 1)
                for i in range(NB):
                    wait_apart(dve, "top_ready", b, i + 1)
                    nc.vector.max_index(top_i[:, i, :], top[:, i, :], logit[:, i, :]).then_inc(s["topi_ready"], 1)
                nc.vector.tensor_tensor(rdiff[:], top[:, :, 1], top[:, :, 0], ALU.subtract).then_inc(s["rdiff_ready"], 1)
                wait(dve, "topi_ready", b, NB)
                nc.vector.tensor_copy(top_f[:], top_i[:, :, 0:2]).then_inc(s["topf_ready"], 1)
                wait(dve, "topf_ready", b, 1)
                for k in range(2):
                    for i in range(NB):
                        last = nc.vector.tensor_scalar(pick[:, k, i, :], ecol, top_f[:, i, k:k + 1], LORA_SCALE, ALU.is_equal, ALU.mult)
                    last.then_inc(s["pick_ready"], 1)
                wait(dve, "rexp_ready", b, 1)
                nc.vector.tensor_scalar(rsum[:], rexp[:], 1.0, None, ALU.add).then_inc(s["rsum_ready"], 1)
                wait(dve, "rsum_ready", b, 1)
                nc.vector.reciprocal(rw[:], rsum[:]).then_inc(s["rw_ready"], 1)
                wait(dve, "rw_ready", b, 1)
                for i in range(NB):
                    last = nc.vector.tensor_scalar(pick[:, 2, i, :], ecol, 0.0, rw[:, i:i + 1], ALU.mult, ALU.add)
                last.then_inc(s["pick_ready"], 1)
                wait(dve, "u_ps", b, 2)
                wait(dve, "pickT_ready", b, 1)
                for k in range(2):
                    nc.vector.tensor_tensor(um[:, k, :], ps[:, 2 + k, :], pickT[:, 0, :], ALU.mult).then_inc(s["um_ready"], 1)
                wait(dve, "pickd_ready", b, 1)
                for k in range(2):
                    nc.vector.tensor_tensor(um[:, 2 + k, :], ps[:, 2 + k, :], pickw[:, 2, :], ALU.mult).then_inc(s["um_ready"], 1)

                def product(f, slot, dst, name_sil, name_out):
                    wait(dve, name_sil, b, f + 1)
                    if f >= 2:
                        wait(dve, "down_ps", b, f - 1)
                    r = 2 * (f % 2)
                    if f < NF:
                        nc.vector.tensor_tensor(dst[:, f % 2, :], ps[:, r + 1, :], sil[:, slot, :], ALU.mult).then_inc(s[name_out], 1)
                    else:
                        nc.vector.tensor_tensor(dst[0:FT, f % 2, :], ps[FT:2 * FT, r, :], sil[FT:2 * FT, slot, :], ALU.mult).then_inc(s[name_out], 1)

                for f in range(NFT + 1):
                    if f < NFT:
                        product(f, 0, act1, "fa_sil", "fa_act")
                    if f >= 1:
                        product(f - 1, 1, act2, "fb_sil", "fb_act")
                        m = P if f - 1 < NF else FT
                        wait(dve, "gw_ready", b, 2 * f)
                        nc.vector.tensor_tensor(gsum[0:m, (f - 1) % 2, :], gw[0:m, 0, :], gw[0:m, 1, :], ALU.add).then_inc(s["gsum_ready"], 1)
                wait(dve, "down_ps", b, NFT)
                wait(dve, "gsum_ready", b, NFT)
                wait(dve, "pickw_ready", b, 2)
                nc.vector.tensor_tensor(tm[:, 0, :], ps[:, 4, :], pickw[:, 0, :], ALU.mult).then_inc(s["tm_1"], 1)
                nc.vector.tensor_tensor(tm[:, 1, :], ps[:, 5, :], pickw[:, 1, :], ALU.mult).then_inc(s["tm_2"], 1)
                wait(dve, "tm_2", b, 1)
                nc.vector.tensor_tensor(tm[:, 0, :], tm[:, 0, :], tm[:, 1, :], ALU.add).then_inc(s["tm_ready"], 1)
                for i in range(NB):
                    wait(dve, "o_ps", b, i // 2 * 2 + 2)
                    if i >= 1:
                        wait(dve, "o_ready", b, i)
                    nc.vector.tensor_tensor(osb[:], ps[:, 6 + i // 2, (i % 2) * D:(i % 2 + 1) * D], gates[:, b, 1, :], ALU.mult).then_inc(s["o_gated"], 1)
                    wait(dve, "o_gated", b, i + 1)
                    nc.vector.tensor_tensor(xs[:, b * NB + i, :], xs[:, b * NB + i, :], osb[:], ALU.add).then_inc(s["o_ready"], 1)

            dve.wait_ge(s["small_in"], 80)
            nc.vector.tensor_copy(slope_p[:, 0:1], slope[:]).then_inc(s["sl_1"], 1)
            dve.wait_ge(s["sl_1"], 1)
            nc.vector.tensor_tensor(slope_r[:, 0:1], slope[:], slope_p[:, 0:1], ALU.subtract).then_inc(s["sl_2"], 1)
            dve.wait_ge(s["sl_2"], 1)
            nc.vector.tensor_copy(slope_p[:, 1:2], slope_r[:, 0:1]).then_inc(s["sl_3"], 1)
            dve.wait_ge(s["sl_3"], 1)
            nc.vector.tensor_tensor(slope_p[:, 2:3], slope_r[:, 0:1], slope_p[:, 1:2], ALU.subtract).then_inc(s["sl_4"], 1)
            dve.wait_ge(s["sl_4"], 1)
            dve.wait_ge(s["const_in"], 16)
            for i in range(3):
                for sign in (1.0, -1.0):
                    nc.vector.tensor_scalar(slope_w[:, i if sign > 0 else 3 + i, :], slope_p[:, i:i + 1].to_broadcast([H, S]),
                                            sign, None, ALU.mult).then_inc(s["slope_wide"], 1)
            nc.vector.tensor_scalar(b_qk[:, 0:KT], b_qk[:, 0:KT], SCALE, None, ALU.mult).then_inc(s["bq_scaled"], 1)
            nc.vector.tensor_copy(ident_b[:], ident).then_inc(s["const_ready"], 1)
            nc.vector.tensor_copy(kmask_b[:], kmask).then_inc(s["const_ready"], 1)
            dve.wait_ge(s["x_in"], 32)
            dve.wait_ge(s["zero_done"], 5)
            dve.wait_ge(s["const_ready"], 2)
            dve.wait_ge(s["bq_scaled"], 1)
            front(0, first=True)
            for b in range(B):
                dve.wait_ge(s["gate_ps"], b + 1)
                if b:
                    dve.wait_ge(s["gates_ready"], b)
                g = ps[:, 6 + b % 2, :]
                nc.vector.tensor_scalar(g_abs, g, -1.0, None, ALU.mult).then_inc(s["gate_neg"], 1)
                dve.wait_ge(s["gate_neg"], b + 1)
                nc.vector.tensor_tensor(g_abs, g, g_abs, ALU.max).then_inc(s["gate_abs"], 1)
                nc.vector.tensor_scalar(g_sgn, g, 0.0, 2.0, ALU.is_ge, ALU.mult).then_inc(s["gate_sgn"], 1)
                dve.wait_ge(s["gate_sgn"], b + 1)
                nc.vector.tensor_scalar(g_abs, g_abs, GATE_FLOOR, None, ALU.max).then_inc(s["gate_floor"], 1)
                dve.wait_ge(s["gate_floor"], b + 1)
                nc.vector.scalar_tensor_tensor(out=gates[:, b].rearrange("p a d -> p (a d)"), in0=g_sgn, scalar=-1.0, in1=g_abs,
                                               op0=ALU.add, op1=ALU.mult).then_inc(s["gates_ready"], 1)
            dve.wait_ge(s["gates_ready"], B)
            with dve.Fori(0, B - 1) as b:
                attention(b)
                front(b + 1)
                ffn(b)
            attention(B - 1)
            ffn(B - 1)

        @block.tensor
        def _(pe):
            mm = nc.tensor.matmul

            def transposes(b, n, bank):
                for k in range(KT):
                    for i in range(NB):
                        wait(pe, f"ln{n}_xhat", b, i + 1)
                        last = nc.tensor.transpose(ps[:, bank + k, i * P:(i + 1) * P], xhat[:, i, k * P:(k + 1) * P], ident)
                    last.then_inc(s[f"h{n}T_ps"], 1)

            def front(b):
                transposes(b, 1, 4)
                wait(pe, "h1T_ready", b, KT)
                for t in range(NQK):
                    for k in range(KT):
                        last = mm(ps[:, t, :], wqkv[:, k, t * P:(t + 1) * P], hT[:, k, :], start=k == 0, stop=k == KT - 1)
                    last.then_inc(s["qk_ps"], 1)
                for i in range(NB):
                    for k in range(KT):
                        last = mm(ps[:, 4 + i // 2, (i % 2) * D:(i % 2 + 1) * D], hT[:, k, i * P:(i + 1) * P],
                                  wqkv[:, k, 2 * D:3 * D], start=k == 0, stop=k == KT - 1)
                    last.then_inc(s["v_ps"], 1)

            def attention(b):
                wait(pe, "rows_landed", b, per["rows_landed"])
                wait(pe, "v_ready", b, NB)
                freed = {}
                for kind, h, n in steps:
                    base = (n % 2) * 1536
                    if kind in ("p1", "p2"):
                        if n >= 2:
                            was, i = tasks[n - 2]
                            wait(pe, "p1_done" if was == "p1" else "p2_exp", b, i + 1)
                    if kind == "p1":
                        for i in (3, 2, 0, 1):
                            a = base + START1[i]
                            last = mm(psb[:, a:a + WIDTH1[i]], QA[0:R_NORM, h, i * P:(i + 1) * P], KA[0:R_NORM, h, 0:WIDTH1[i]],
                                      start=True, stop=True)
                        last.then_inc(s["p1_ps"], 1)
                    elif kind == "norm_t":
                        wait_apart(pe, "lse_parts", b, h + 1)
                        if h >= 1:
                            wait(pe, "lse_evac", b, h)
                        nc.tensor.transpose(ps[:, 7, :].bitcast(BF16)[0:3 * G * NB, 0:P], lse_p[:].rearrange("p c n -> p (c n)"),
                                            ident_b[:]).then_inc(s["lse_ps"], 1)
                    elif kind == "p2":
                        if h % G == 0:
                            wait(pe, "lse_landed", b, 48 * (h // G + 1))
                        for j in (0, 1, 3, 2):
                            a = base + START2[j]
                            mm(psb[:, a:a + P], ident_b[:], kmask_b[:], start=True, stop=True)
                            last = mm(psb[:, a:a + WIDTH2[j]], KA[0:R_ALL, h, j * P:(j + 1) * P], QA[0:R_ALL, h, j * P:S],
                                      start=False, stop=True, skip_group_check=True)
                        last.then_inc(s["p2_ps"], 1)
                    elif kind == "pv":
                        wait(pe, "p2_ready", b, G * (h + 1))
                        if h == 0:
                            wait(pe, "vsuf_ready", b, 1)
                        else:
                            wait(pe, "att_ready", b, h)
                        for i in range(NB - 1):
                            for c in range(G):
                                hh = G * h + c
                                v = V[:, 3, hh, :] if i == 2 else Vsuf[:, i, hh, :]
                                mm(ps[32 * c:32 * c + 32, 6, i * P:(i + 1) * P], v, floor_c[:], start=i == 0, stop=True,
                                   skip_group_check=True)
                        for j in (3, 2, 1, 0):
                            for c in range(G):
                                hh = G * h + c
                                last = mm(ps[32 * c:32 * c + 32, 6, j * P:S], V[:, j, hh, :],
                                          prob[:, hh % NPROB, START2[j]:START2[j] + WIDTH2[j]], start=False, stop=True,
                                          skip_group_check=True)
                        last.then_inc(s["pv_ps"], 1)
                wait(pe, "att_ready", b, NG)
                wait(pe, "lse_evac", b, NG)
                for i in range(NB):
                    for g in range(NG):
                        last = mm(ps[:, 6 + i // 2, (i % 2) * D:(i % 2 + 1) * D], att[:, g, i * P:(i + 1) * P], wo[:, g, :],
                                  start=g == 0, stop=g == NG - 1)
                    last.then_inc(s["y_ps"], 1)

            def ffn(b):
                transposes(b, 2, 6)
                wait(pe, "h2T_ready", b, KT)
                wait(pe, "v_ready", b + 1, NB) if not isinstance(b, int) else None
                for i in range(NB):
                    for k in range(KT):
                        last = mm(ps[:, 4, i * E:(i + 1) * E], h2T[:, k, i * P:(i + 1) * P], gate_w[:, k, :], start=k == 0, stop=k == KT - 1)
                last.then_inc(s["logit_ps"], 1)
                wait(pe, "qk_evac", b + 1, NQK) if not isinstance(b, int) else None
                for t in range(2):
                    for k in range(KT):
                        last = mm(ps[:, 2 + t, :], a13[:, k, t * P:(t + 1) * P], h2T[:, k, :], start=k == 0, stop=k == KT - 1)
                    last.then_inc(s["u_ps"], 1)

                def targets(f):
                    c0, m = tile_cols(f)
                    r = 2 * (f % 2)
                    if f < NF:
                        return [(ps[:, r, :], c0), (ps[:, r + 1, :], c0 + P)]
                    return [(ps[:, r, :], c0)]

                def base(f):
                    if f >= 2:
                        wait(pe, "fb_act", b, f - 1)
                    for dst, c0 in targets(f):
                        for k in range(KT):
                            mm(dst, w13[:, k, c0:c0 + P], h2T[:, k, :], start=k == 0, stop=k == KT - 1)

                def lora(f, slot):
                    if slot == 1:
                        wait(pe, "fa_act", b, f + 1)
                    for n, (dst, c0) in enumerate(targets(f)):
                        if f < NF:
                            last = mm(dst, b13[:, c0:c0 + P], um[:, 2 * slot + n, :], start=False, stop=True, skip_group_check=True)
                        else:
                            for q in range(2):
                                last = mm(dst[q * FT:(q + 1) * FT], b13[:, c0 + q * FT:c0 + (q + 1) * FT], um[:, 2 * slot + q, :],
                                          start=False, stop=True, skip_group_check=True)
                    last.then_inc(s["fb_ps" if slot else "fa_ps"], 1)

                def down(f):
                    wait(pe, "gsum_ready", b, f + 1)
                    if f == 0:
                        wait(pe, "pickT_ready", b, 4)
                    mm(ps[:, 4, :], a2[:, f, :], act1[:, f % 2, :], start=f == 0, stop=f == NFT - 1)
                    mm(ps[:, 5, :], a2[:, f, :], act2[:, f % 2, :], start=f == 0, stop=f == NFT - 1)
                    for i in range(NB):
                        last = mm(ps[:, 6 + i // 2, (i % 2) * D:(i % 2 + 1) * D], gsum[:, f % 2, i * P:(i + 1) * P], w2[:, f, :],
                                  start=f == 0 and i % 2 == 0, stop=True, skip_group_check=True)
                    last.then_inc(s["down_ps"], 1)

                base(0)
                for k, bank in ((0, 6), (1, 7), (2, 5)):
                    wait(pe, "pick_ready", b, k + 1)
                    for i in range(NB):
                        last = nc.tensor.transpose(ps[:, bank, i * P:(i + 1) * P], pick[:, k, i, :], ident)
                    last.then_inc(s["pick_ps"], 1)
                wait(pe, "um_ready", b, 2)
                lora(0, 0)
                wait(pe, "um_ready", b, 4)
                for f in range(1, NFT + 2):
                    if f < NFT:
                        base(f)
                        lora(f, 0)
                    if f - 1 < NFT:
                        lora(f - 1, 1)
                    if f >= 2:
                        down(f - 2)
                wait(pe, "tm_ready", b, 1)
                for i in range(NB):
                    mm(ps[:, 6 + i // 2, (i % 2) * D:(i % 2 + 1) * D], tm[:, 0, i * P:(i + 1) * P], b2[:], start=False, stop=True,
                       skip_group_check=True).then_inc(s["o_ps"], 1)

            pe.wait_ge(s["const_ready"], 2)
            pe.wait_ge(s["wmod_in"], 16)
            pe.wait_ge(s["cs_ready"], 1)
            for a, chunk in enumerate((0, 1, 3, 4)):
                for t in range(KT):
                    for k in range(KT):
                        last = mm(ps[:, 0, (a * KT + t) * B:(a * KT + t + 1) * B], wmod_s[:, k, chunk * D + t * P:chunk * D + (t + 1) * P],
                                  c_silu[:, k, :], start=k == 0, stop=k == KT - 1)
            last.then_inc(s["mod_ps"], 1)
            pe.wait_ge(s["wqkv_in"], 16)
            pe.wait_ge(s["modt_ready"], 4)
            front(0)
            pe.wait_ge(s["cwide_ready"], 1)
            for b in range(B):
                if b >= 2:
                    pe.wait_ge(s["gates_ready"], b - 1)
                for n, chunk in enumerate((2, 5)):
                    for k in range(KT):
                        last = mm(ps[:, 6 + b % 2, n * D:(n + 1) * D], c_wide[:, k, b, :], wmod_s[:, k, chunk * D:(chunk + 1) * D],
                                  start=k == 0, stop=k == KT - 1)
                last.then_inc(s["gate_ps"], 1)
            pe.wait_ge(s["rows_in"], 16 * 15)
            pe.wait_ge(s["out_w_in"], 64)
            pe.wait_ge(s["ffn_in"], 128)
            pe.wait_ge(s["small_in"], 80)
            pe.wait_ge(s["gates_ready"], B)
            with pe.Fori(0, B - 1) as b:
                attention(b)
                front(b + 1)
                ffn(b)
            attention(B - 1)
            ffn(B - 1)


_OUT = (4, 512, 256)


def kernel(L0_attn_qkv, L0_attn_in_proj, L0_attn_in_proj_bias, L0_attn_out_w, L0_attn_out_b, L0_attn_alibi_slopes, L0_ffn_gate_w,
           L0_ffn_w1, L0_ffn_w3, L0_ffn_w2, L0_ffn_a1, L0_ffn_b1, L0_ffn_a3, L0_ffn_b3, L0_ffn_a2, L0_ffn_b2, L0_c, L0_wmod):
    import numpy as np
    import ml_dtypes
    import concourse.bacc as bacc
    from concourse.bass_utils import run_bass_kernel_spmd

    a = {k: np.asarray(v) for k, v in dict(
        x=L0_attn_qkv, in_proj=L0_attn_in_proj, bqkv=L0_attn_in_proj_bias, out_w=L0_attn_out_w, bo=L0_attn_out_b,
        slopes=L0_attn_alibi_slopes, gate=L0_ffn_gate_w, w1=L0_ffn_w1, w3=L0_ffn_w3, w2=L0_ffn_w2, a1=L0_ffn_a1, b1=L0_ffn_b1,
        a3=L0_ffn_a3, b3=L0_ffn_b3, a2=L0_ffn_a2, b2=L0_ffn_b2, c=L0_c, wmod=L0_wmod).items()}
    E, R, D = a["a1"].shape
    F = a["w1"].shape[0]

    def pair(u, v):
        cuts = list(range(0, F, 128))
        return np.concatenate([m[:, n:n + 128] for n in cuts for m in (u, v)], axis=1)

    def ranks(w):
        return w.transpose(0, 2, 1).reshape(E * R, w.shape[1])

    n = np.arange(128)
    consts = np.zeros((128, 896), np.float32)
    consts[:, 0:128] = np.eye(128)
    consts[:, 128 + 384:640] = np.where(n[None, :] > n[:, None], MASKED, 0.0)
    consts[:, 640:768] = np.where(n[:, None] > n[None, :], MASKED, 0.0)
    consts[:, 768:896] = n[None, :] // R
    pos = np.ones((2, 1, 16, 512), np.float32)
    pos[0] = np.arange(512) - 256
    arrays = dict(
        x=a["x"], wqkvT=a["in_proj"].T, bqk=a["bqkv"][:2 * D].reshape(-1, 128).T, bv=a["bqkv"][2 * D:], woT=a["out_w"].T, bo=a["bo"], slopes=a["slopes"], gateT=a["gate"].T,
        w13T=pair(a["w1"].T, a["w3"].T), w2T=a["w2"].T, a13T=np.concatenate([a["a1"].reshape(E * R, D).T, a["a3"].reshape(E * R, D).T], axis=1),
        b13T=pair(ranks(a["b1"]), ranks(a["b3"])), a2T=a["a2"].reshape(E * R, F).T, b2T=ranks(a["b2"]), cT=a["c"].T, wmod=a["wmod"],
        consts=consts, pos_rows=pos.astype(ml_dtypes.bfloat16))
    nc = bacc.Bacc("TRN2", target_bir_lowering=False, num_devices=1)
    feed, args = {}, []
    for name, v in arrays.items():
        v = np.ascontiguousarray(v)
        feed[f"in_{name}"] = v
        args.append(nc.dram_tensor(f"in_{name}", v.shape, mybir.dt.from_np(v.dtype), kind="ExternalInput").ap())
    args.append(nc.dram_tensor("result", _OUT, F32, kind="ExternalOutput").ap())
    adaln_block(nc, *args)
    return run_bass_kernel_spmd(nc, [feed], core_ids=[0]).results[0]["result"]
```

```python
from contextlib import ExitStack

import concourse.bass as bass
from concourse import mybir

P = 128
ALU = mybir.AluOpType
ACT = mybir.ActivationFunctionType
BF16 = mybir.dt.bfloat16
F32 = mybir.dt.float32
U32 = mybir.dt.uint32

LN_EPS = 1e-5
GATE_FLOOR = 0.25
PROB_FLOOR = 1e-10
LORA_SCALE = 2.0
MASKED = -3e38
LN_SLOPE = 0.6931471805599453 / 2 ** 23
LN_AT_ZERO = (127 - 0.043) * 0.6931471805599453


def adaln_block(nc, x, wqkvT, bqk, bv, woT, bo, slopes, gateT, w13T, w2T, a13T, b13T, a2T, b2T, cT, wmod,
                consts, pos_rows, out):
    B, S, D = x.shape
    H = slopes.shape[0]
    DH = D // H
    F = w2T.shape[0]
    E = gateT.shape[1]
    KT = D // P
    NB = S // P
    G = 4
    NG = H // G
    NF = F // P
    FT = F - NF * P
    NFT = NF + 1
    NQK = 2 * KT
    SCALE = float(DH) ** -0.5
    assert (B, S, D, H, F, E) == (4, 512, 256, 16, 704, 8) and FT == 64 and b13T.shape[0] == P

    R_SLOPE = 6 * DH
    R_POS = R_SLOPE + 3
    R_NORM = R_SLOPE + 6
    R_ALL = R_SLOPE + 9
    Q_PART = (0, 0, 1, 0, 1, 2)
    K_PART = (0, 1, 0, 2, 1, 0)

    WIDTH1, WIDTH2 = (128, 256, 384, 512), (512, 384, 256, 128)
    START2 = (0, 512, 1024, 896)
    COLS = 1280

    def pair_units(kind, p):
        h = 2 * p
        if kind == "p1":
            return [[(h, 3, 0)], [(h, 2, 0), (h, 0, 384)], [(h + 1, 3, 0)], [(h + 1, 2, 0), (h + 1, 0, 384)], [(h, 1, 0), (h + 1, 1, 256)]]
        return [[(h, 0, 0)], [(h, 1, 0), (h, 3, 384)], [(h + 1, 0, 0)], [(h + 1, 1, 0), (h + 1, 3, 384)], [(h, 2, 0), (h + 1, 2, 256)]]

    PAIRS, LEAD = H // 2, 4
    UNITS = 5
    RING = 3
    units = []
    for p in range(PAIRS + LEAD):
        p2 = [("p2", (p - LEAD) * UNITS + i, u) for i, u in enumerate(pair_units("p2", p - LEAD))] if p >= LEAD else []
        p1 = [("p1", p * UNITS + i, u) for i, u in enumerate(pair_units("p1", p))] if p < PAIRS else []
        if p1 and p2:
            units += [u for both in zip(p2, p1) for u in both]
        else:
            units += p1 + p2
    place = {(kind, i): n for n, (kind, i, _) in enumerate(units)}
    NS = 2 * NFT
    HS = S // 2

    def attention_steps(engine):
        late = {"act": {"p1": 1.1, "p2": 0.4}, "dve": {"p1": 0.5}}.get(engine, {})
        steps = []
        for n, (kind, i, parts) in enumerate(units):
            if engine in ("pe", "act") or kind == "p1":
                steps.append((n + late.get(kind, 0), kind, (n, i, parts)))
        for p in range(PAIRS):
            end1, end2 = place["p1", UNITS * p + 4], place["p2", UNITS * p + 4]
            if engine == "dve":
                steps.append((end2 + 1.0, "floor", p))
            if p % 2:
                g = p // 2
                if engine in ("act", "dve"):
                    steps.append((end1 + (1.3 if engine == "act" else 1.2), "norm", g))
                steps.append((end1 + {"pe": 4.6, "act": 5.2, "sp": 5.3, "dve": 1.7}[engine], "norm_t", g))
                steps.append((end2 + {"pe": 3.6, "act": 5.3, "sp": 4.0, "dve": 1.2}[engine], "pv", g))
        steps.append((len(units) + 8, "y", 0))
        return steps

    def ffn_steps(engine, alone):
        steps = []
        for n in range(NS):
            if alone:
                base, second, down = 2.0 * n, 2.0 * (n + 1) + 0.1, 2.0 * (n + 2) + 0.6
            else:
                base = (-8, -5, 0.5)[n] if n < 3 else 0.5 + 7.9 * (n - 2)
                second, down = base + 3.4, base + 8.3
            steps.append((base, "base", n))
            steps.append((base + (0.2 if engine == "pe" else 0.7), "first", n))
            steps.append((second + (0 if engine == "pe" else 0.5), "second", n))
            steps.append((down, "down", n))
            if n % NFT == NFT - 1:
                steps.append((down + (0.5 if alone else 0.3), "weigh", n // NFT))
                steps.append((down + (0.7 if alone else 1.3), "result", n // NFT))
        return steps

    def merged(engine, attention, ffn):
        return sorted((attention_steps(engine) if attention else []) + (ffn_steps(engine, not attention) if ffn else []),
                      key=lambda step: step[0])

    with ExitStack() as ctx:
        def sb(name, shape, dt=F32):
            return ctx.enter_context(nc.sbuf_tensor(name, shape, dt))

        ps = ctx.enter_context(nc.psum_tensor("ps", [P, 8, 512], F32))
        ATT_BANK, FFN_BANK, T_BANK, OUT_BANK = 3, 4, 6, 7
        scratch = nc.dram_tensor("qk_scratch", (NQK * P, 3, S), BF16, kind="Internal").ap()

        const = sb("const", [P, 896])
        ident, qmask, kmask, ecol = const[:, 0:128], const[:, 128:640], const[:, 640:768], const[:, 768:896]
        ident_b, kmask_b = sb("ident_b", [P, P], BF16), sb("kmask_b", [P, P], BF16)
        floor_c, half_c = sb("floor_c", [P, P]), sb("half_c", [P, 1])
        wqkv = sb("wqkv", [P, KT, 3 * D])
        wo = sb("wo", [P, NG, D])
        w13 = sb("w13", [P, KT, 2 * F])
        b13 = sb("b13", [P, 2 * F])
        a13 = sb("a13", [P, KT, 2 * P])
        w2, a2, b2 = sb("w2", [P, NFT, D]), sb("a2", [P, NFT, P]), sb("b2", [P, D])
        gate_w = sb("gate_w", [P, KT, E])
        b_qk, b_v, b_o = sb("b_qk", [P, NQK]), sb("b_v", [P, D]), sb("b_o", [P, D])
        c_t, c_silu = sb("c_t", [P, KT, B]), sb("c_silu", [P, KT, B])
        mod_t = sb("mod_t", [P, 4, KT, B])
        gates = sb("gates", [P, B, 2, D])
        slope, slope_r = sb("slope", [H, 1]), sb("slope_r", [H, 2])
        slope_p = sb("slope_p", [H, 3], BF16)

        xs = sb("xs", [P, B * NB, D])
        stats = sb("stats", [P, (B - 1) * NB, 6])
        mv1, rstd1 = sb("mv1", [P, B * NB, 2]), sb("rstd1", [P, B * NB])
        mv2, rstd2 = sb("mv2", [P, NB, 2]), sb("rstd2", [P, NB])
        veps, vbits, logv, rstd0, ra, re = [sb(n, [P, (B - 1) * NB]) for n in ("veps", "vbits", "logv", "rstd0", "ra", "re")]
        mv_now, rstd_now = sb("mv_now", [P, NB, 1]), sb("rstd_now", [P, NB])
        xhat1, xhat2 = sb("xhat1", [P, NB, D]), sb("xhat2", [P, NB, D])
        modc = sb("modc", [P, 2, 2, KT])
        hT, h2T = sb("hT", [P, KT, S]), sb("h2T", [P, KT, S])
        QA, KA = sb("QA", [P, H, S], BF16), sb("KA", [P, H, S], BF16)
        V, Vsuf = sb("V", [P, NB, H, 32]), sb("Vsuf", [P, 2, H, 32])
        shift, zsum = sb("shift", [P, H, NB]), sb("zsum", [P, H, NB])
        zbits, logz, zinv = sb("zbits", [P, G * NB]), sb("logz", [P, G * NB]), sb("zinv", [P, G * NB])
        za, ze = sb("za", [P, G * NB]), sb("ze", [P, G * NB])
        lse, lse_r = sb("lse", [P, G * NB]), sb("lse_r", [P, G * NB])
        lse_p, lse_t = sb("lse_p", [P, 3, G * NB], BF16), sb("lse_t", [3 * G * NB, P], BF16)
        NPROB = 6
        prob = sb("prob", [P, NPROB, COLS])
        att = sb("att", [P, NG, S])
        ysb, osb = sb("ysb", [P, D]), sb("osb", [P, D])
        early = prob[:].rearrange("p g n -> p (g n)")
        qk_p = early[:, 0:NQK * 3 * S // 2].bitcast(BF16).rearrange("p (t c n) -> p t c n", t=NQK, c=3)
        qk_f = early[:, 3072:3072 + 2 * S].rearrange("p (t n) -> p t n", t=2)
        qk_r = early[:, 4096:4096 + S]
        pick = early[:, 4608:4608 + 3 * S].rearrange("p (k i n) -> p k i n", k=3, i=NB)
        slope_w = early[0:H, 6144:7680].bitcast(BF16).rearrange("p (k n) -> p k n", k=6)

        logit, top, top_i = sb("logit", [P, NB, E]), sb("top", [P, NB, 8]), sb("top_i", [P, NB, 8], U32)
        top_f = sb("top_f", [P, NB, 2])
        rdiff, rexp, rsum, rw = sb("rdiff", [P, NB]), sb("rexp", [P, NB]), sb("rsum", [P, NB]), sb("rw", [P, NB])
        route = sb("route", [P, 11 * S])
        pickT = route[:, 0:4 * S].rearrange("p (k n) -> p k n", k=4)
        pickw = route[:, 4 * S:7 * S].rearrange("p (k n) -> p k n", k=3)
        um = route[:, 7 * S:11 * S].rearrange("p (k n) -> p k n", k=4)
        wmod_s = route[:, 0:KT * 6 * D].rearrange("p (k n) -> p k n", k=KT)
        c_wide = route[:, 3072:3072 + KT * B * P].rearrange("p (k b n) -> p k b n", k=KT, b=B)
        g_abs, g_sgn = route[:, 4096:4608], route[:, 4608:5120]
        sil, gw, tm = sb("sil", [P, 2, HS]), sb("gw", [P, 2, HS]), sb("tm", [P, 2, HS])
        act1, act2, gsum = sb("act1", [P, 2, HS]), sb("act2", [P, 2, HS]), sb("gsum", [P, 2, HS])

        per = dict(
            ln1_now=2, ln1_xhat=NB, h1T_ps=KT, h1T_ready=KT,
            ln2_stat=NB, ln2_aggr=NB, ln2_veps=1, ln2_bits=1, ln2_log=1, ln2_seed=1, ln2_poly=8, ln2_xhat=NB, h2T_ps=KT, h2T_ready=KT,
            mod1_now=1, mod2_now=1, qk_ps=NQK, qk_evac=NQK, qk_hi=NQK, qk_res=NQK, qk_mid=NQK, qk_parts=NQK, v_ps=NB, v_ready=NB,
            vsuf_mid=1, vsuf_ready=1, q_out=16, k_out=16, rows_landed=16 * 12,
            p1_ps=UNITS * PAIRS, p1_max=UNITS * PAIRS, p1_done=UNITS * PAIRS, zbits_ready=NG, log_ready=NG, lse_first=NG, zinv_ready=NG,
            log_poly=6 * NG, lse_ready=NG, lse_hi=NG, lse_res=NG, lse_mid=NG, lse_parts=NG,
            lse_ps=NG, lse_evac=NG, lse_landed=48 * NG, p2_ps=UNITS * PAIRS, p2_exp=UNITS * PAIRS, p2_ready=PAIRS, pv_ps=NG, att_ready=NG,
            y_ps=NB, y_biased=NB, y_gated=NB, x1_ready=NB,
            logit_ps=1, logit_ready=1, top_ready=NB, topi_ready=NB, topf_ready=1, rdiff_ready=1, rexp_ready=1,
            rsum_ready=1, rw_ready=1, pick_ready=3, pick_ps=3, pickT_ready=4, pickd_ready=1, pickw_ready=2, u_ps=2, um_ready=4,
            fa_ps=NS, fa_tanh=NS, fa_gate=NS, fa_act=NS, fb_ps=NS, fb_tanh=NS, fb_gate=NS, fb_act=NS, gw_ready=2 * NS, gsum_ready=NS,
            down_ps=NS, tm_1=2, tm_2=2, tm_ready=2, o_ps=NB, o_gated=NB, o_ready=NB, store_done=16 * NB)
        for first in ("ln1a", "ln1b"):
            blocks = NB if first == "ln1a" else (B - 1) * NB
            per.update({f"{first}_stat": blocks, f"{first}_aggr": blocks, f"{first}_veps": 1, f"{first}_bits": 1, f"{first}_log": 1,
                        f"{first}_seed": 1, f"{first}_poly": 8})
        once = """const_in x_in c_in wmod_in wqkv_in small_in rows_in out_w_in zero_done ffn_in cs_ready cwide_ready
            mod_ps mod_evac modt_ready gate_ps gate_abs gate_sgn gate_neg gate_floor gates_ready sl_1 sl_2 sl_3 sl_4 sl_5
            slope_wide bq_scaled const_ready""".split()
        s = {n: ctx.enter_context(nc.semaphore(n)) for n in [*per, *once]}
        block = ctx.enter_context(nc.Block())

        def wait(eng, name, b, k):
            eng.wait_ge(s[name], b * per[name] + k)

        def wait_apart(eng, name, b, k):
            value = b * per[name] + k
            if not isinstance(b, int):
                value = eng.to_reg(value)
            eng.wait_ge(s["const_ready"], 2)
            eng.wait_ge(s[name], value)

        def tile_cols(f):
            return (f * 2 * P, P) if f < NF else (NF * 2 * P, FT)

        def of_step(n):
            f, half = n % NFT, n // NFT
            return f, slice(half * HS, (half + 1) * HS), FFN_BANK + n % 2, n % 2, P if f < NF else FT

        @block.sync
        def _(sp):
            def load(dst, src, name):
                sp.dma_start(dst, src).then_inc(s[name], 16)

            xv = x.rearrange("b (i p) d -> p (b i) d", p=P)
            load(xs[:, 0:NB, :], xv[:, 0:NB, :], "x_in")
            load(c_t[:], cT.rearrange("(k p) b -> p k b", p=P), "c_in")
            load(const[:], consts, "const_in")
            load(wqkv[:], wqkvT.rearrange("(k p) n -> p k n", p=P), "wqkv_in")
            load(b_qk[:], bqk, "small_in")
            load(b_v[:], bv.rearrange("(o d) -> o d", o=1).to_broadcast([P, D]), "small_in")
            load(b_o[:], bo.rearrange("(o d) -> o d", o=1).to_broadcast([P, D]), "small_in")
            load(slope[:], slopes.rearrange("(h o) -> h o", o=1), "small_in")
            load(gate_w[:], gateT.rearrange("(k p) e -> p k e", p=P), "small_in")
            for i in range(3):
                load(QA[R_POS + i:R_POS + i + 1, :, :], pos_rows[0], "rows_in")
                load(KA[R_SLOPE + i:R_SLOPE + i + 1, :, :], pos_rows[0], "rows_in")
                load(KA[R_NORM + i:R_NORM + i + 1, :, :], pos_rows[1], "rows_in")
            load(xs[:, NB:, :], xv[:, NB:, :], "x_in")
            sp.wait_ge(s["slope_wide"], 6)
            for i in range(3):
                load(QA[R_SLOPE + i:R_SLOPE + i + 1, :, :], slope_w[:, i, :], "rows_in")
                load(KA[R_POS + i:R_POS + i + 1, :, :], slope_w[:, 3 + i, :], "rows_in")

            def regroup(b):
                for side, name in ((0, "q_out"), (1, "k_out")):
                    wait(sp, "qk_parts", b, (side + 1) * KT)
                    sp.dma_start(scratch[side * D:(side + 1) * D].rearrange("(t p) c q -> p t c q", p=P),
                                 qk_p[:, side * KT:(side + 1) * KT, :, :]).then_inc(s[name], 16)
                for side, name, dst, parts in ((0, "q_out", QA, Q_PART), (1, "k_out", KA, K_PART)):
                    wait(sp, name, b, 16)
                    src = scratch[side * D:(side + 1) * D].rearrange("(h d) c q -> d h c q", d=DH)
                    for r, part in enumerate(parts):
                        sp.dma_start(dst[r * DH:(r + 1) * DH, :, :], src[:, :, part, :]).then_inc(s["rows_landed"], 16)

            def run(ba, bf):
                for _, kind, n in merged("sp", ba is not None, bf is not None):
                    if kind == "norm_t":
                        wait(sp, "lse_evac", ba, n + 1)
                        for i in range(3):
                            sp.dma_start(QA[R_NORM + i:R_NORM + i + 1, n * G:(n + 1) * G, :],
                                         lse_t[i * G * NB:(i + 1) * G * NB, :]).then_inc(s["lse_landed"], 16)
                    elif kind == "result":
                        for i in (2 * n, 2 * n + 1):
                            wait(sp, "o_ready", bf, i + 1)
                            sp.dma_start(out[bf, i * P:(i + 1) * P, :], xs[:, bf * NB + i, :]).then_inc(s["store_done"], 16)

            regroup(0)
            run(0, None)
            with sp.Fori(0, B - 1) as b:
                regroup(b + 1)
                run(b + 1, b)
            run(None, B - 1)
            sp.wait_ge(s["store_done"], B * per["store_done"])

        @block.gpsimd
        def _(pool):
            def load(dst, src, name):
                pool.dma_start(dst, src).then_inc(s[name], 16)

            load(wmod_s, wmod.rearrange("(k p) n -> p k n", p=P), "wmod_in")
            nc.gpsimd.memset(V[:], 0.0).then_inc(s["zero_done"], 1)
            nc.gpsimd.memset(wo[:], 0.0).then_inc(s["zero_done"], 1)
            nc.gpsimd.memset(w2[:], 0.0).then_inc(s["zero_done"], 1)
            nc.gpsimd.memset(a2[:], 0.0).then_inc(s["zero_done"], 1)
            nc.gpsimd.memset(floor_c[:], PROB_FLOOR).then_inc(s["zero_done"], 1)
            nc.gpsimd.memset(half_c[:], 0.5).then_inc(s["zero_done"], 1)
            pool.wait_ge(s["zero_done"], 4)
            wov = woT.rearrange("(g c d) n -> c d g n", c=G, d=DH)
            for c in range(G):
                load(wo[32 * c:32 * c + DH, :, :], wov[c], "out_w_in")
            load(w13[:], w13T.rearrange("(k p) n -> p k n", p=P), "ffn_in")
            load(b13[:], b13T, "ffn_in")
            load(a13[:], a13T.rearrange("(k p) n -> p k n", p=P), "ffn_in")
            load(w2[:, 0:NF, :], w2T[0:NF * P].rearrange("(f p) n -> p f n", p=P), "ffn_in")
            load(w2[0:FT, NF, :], w2T[NF * P:F], "ffn_in")
            load(a2[:, 0:NF, :], a2T[0:NF * P].rearrange("(f p) n -> p f n", p=P), "ffn_in")
            load(a2[0:FT, NF, :], a2T[NF * P:F], "ffn_in")
            load(b2[:], b2T, "ffn_in")

            def front(b):
                wait(pool, "v_ready", b, NB)
                nc.gpsimd.tensor_tensor(Vsuf[:, 1], V[:, 2], V[:, 3], ALU.add).then_inc(s["vsuf_mid"], 1)
                wait(pool, "vsuf_mid", b, 1)
                nc.gpsimd.tensor_tensor(Vsuf[:, 0], V[:, 1], Vsuf[:, 1], ALU.add).then_inc(s["vsuf_ready"], 1)

            def routing(b):
                wait(pool, "pickT_ready", b, 2)
                nc.gpsimd.tensor_tensor(pickw[:, 2, :], pickT[:, 1, :], pickT[:, 0, :], ALU.subtract).then_inc(s["pickd_ready"], 1)
                wait(pool, "pickT_ready", b, 4)
                for k in range(2):
                    nc.gpsimd.tensor_tensor(pickw[:, k, :], pickT[:, k, :], pickT[:, 2 + k, :], ALU.mult).then_inc(s["pickw_ready"], 1)

            def ffn(b):
                routing(b)
                for n in range(NS):
                    f, cols, _, turn, m = of_step(n)
                    wait(pool, "fa_act", b, n + 1)
                    if n >= 1:
                        wait(pool, "gsum_ready", b, n)
                    nc.gpsimd.tensor_tensor(gw[0:m, 0, :], act1[0:m, turn, :], pickT[0:m, 2, cols], ALU.mult).then_inc(s["gw_ready"], 1)
                    wait(pool, "fb_act", b, n + 1)
                    nc.gpsimd.tensor_tensor(gw[0:m, 1, :], act2[0:m, turn, :], pickT[0:m, 3, cols], ALU.mult).then_inc(s["gw_ready"], 1)
                    wait(pool, "gw_ready", b, 2 * n + 2)
                    nc.gpsimd.tensor_tensor(gsum[0:m, turn, :], gw[0:m, 0, :], gw[0:m, 1, :], ALU.add).then_inc(s["gsum_ready"], 1)

            front(0)
            with pool.Fori(0, B - 1) as b:
                front(b + 1)
                ffn(b)
            ffn(B - 1)

        @block.scalar
        def _(act):
            def seed(tag, b, cols):
                wait(act, f"{tag}_log", b, 1)
                nc.scalar.activation(rstd0[:, 0:cols], logv[:, 0:cols], ACT.Exp, scale=-0.5).then_inc(s[f"{tag}_seed"], 1)

            def modulate(b, n, dst, bank):
                wait(act, f"mod{n}_now", b, 1)
                for k in range(KT):
                    wait(act, f"h{n}T_ps", b, k + 1)
                    nc.scalar.activation(dst[:, k, :], ps[:, bank + k, :], ACT.Identity, scale=modc[:, n - 1, 1, k:k + 1],
                                         bias=modc[:, n - 1, 0, k:k + 1]).then_inc(s[f"h{n}T_ready"], 1)

            def evacuate_qk(b, t):
                wait(act, "qk_ps", b, t + 1)
                if t >= 2:
                    wait(act, "qk_res", b, t - 1)
                nc.scalar.activation(qk_f[:, t % 2, :], ps[:, (t + 2) % 4, :], ACT.Identity, bias=b_qk[:, t:t + 1],
                                     scale=SCALE if t < KT else 1.0).then_inc(s["qk_evac"], 1)

            def routing(b):
                wait(act, "rdiff_ready", b, 1)
                nc.scalar.activation(rexp[:], rdiff[:], ACT.Exp).then_inc(s["rexp_ready"], 1)
                for k in range(3):
                    bank = (5, 3, 5)[k]
                    wait(act, "pick_ps", b, k + 1)
                    nc.scalar.copy(pickT[:, k, :], ps[:, bank, :]).then_inc(s["pickT_ready"], 1)
                nc.scalar.activation(pickT[:, 3, :], ps[:, 5, :], ACT.Identity, scale=-1.0, bias=half_c[:]).then_inc(s["pickT_ready"], 1)

            def run(ba, bf):
                for _, kind, n in merged("act", ba is not None, bf is not None):
                    if kind == "p1":
                        at, i, parts = n
                        wait(act, "p1_max", ba, i + 1)
                        for h, blk, c in parts:
                            scores = ps[:, at % RING, c:c + WIDTH1[blk]]
                            last = nc.scalar.activation(scores, scores, ACT.Exp, scale=-1.0, bias=shift[:, h, blk:blk + 1],
                                                        accum_out=zsum[:, h, blk:blk + 1])
                        last.then_inc(s["p1_done"], 1)
                    elif kind == "norm":
                        wait(act, "log_ready", ba, n + 1)
                        nc.scalar.activation(zinv[:], logz[:], ACT.Exp, scale=-1.0).then_inc(s["zinv_ready"], 1)
                    elif kind == "norm_t":
                        wait(act, "lse_ps", ba, n + 1)
                        if n >= 1:
                            wait(act, "lse_landed", ba, 48 * n)
                        nc.scalar.copy(lse_t[:], ps[:, ATT_BANK, :].bitcast(BF16)[0:3 * G * NB, 0:P]).then_inc(s["lse_evac"], 1)
                    elif kind == "p2":
                        at, i, parts = n
                        p, u = i // UNITS, i % UNITS
                        slot = 2 * p % NPROB
                        wait(act, "p2_ps", ba, i + 1)
                        if 2 * p >= NPROB:
                            wait(act, "pv_ps", ba, (2 * p - NPROB) // G + 1)
                        if u < 4:
                            nc.scalar.activation(prob[:, slot + u // 2, (u % 2) * 512:(u % 2 + 1) * 512], ps[:, at % RING, :],
                                                 ACT.Exp).then_inc(s["p2_exp"], 1)
                        else:
                            nc.scalar.activation(prob[:, slot:slot + 2, 1024:1280], ps[:, at % RING, :].rearrange("p (h n) -> p h n", h=2),
                                                 ACT.Exp).then_inc(s["p2_exp"], 1)
                    elif kind == "pv":
                        wait(act, "pv_ps", ba, n + 1)
                        nc.scalar.copy(att[:, n, :], ps[:, ATT_BANK, :]).then_inc(s["att_ready"], 1)
                    elif kind in ("first", "second"):
                        f, cols, bank, turn, m = of_step(n)
                        slot, x_ = (0, "fa") if kind == "first" else (1, "fb")
                        wait(act, x_ + "_ps", bf, n + 1)
                        if n >= 1:
                            wait(act, x_ + "_act", bf, n)
                        nc.scalar.activation(sil[0:m, slot, :], ps[0:m, bank, 0:HS], ACT.Tanh, scale=0.5).then_inc(s[x_ + "_tanh"], 1)

            act.wait_ge(s["c_in"], 16)
            nc.scalar.activation(c_silu[:], c_t[:], ACT.Silu).then_inc(s["cs_ready"], 1)
            seed("ln1a", 0, NB)
            modulate(0, 1, hT, 0)
            for t in range(NQK):
                evacuate_qk(0, t)
            seed("ln1b", 0, (B - 1) * NB)
            run(0, None)
            with act.Fori(0, B - 1) as b:
                modulate(b + 1, 1, hT, 0)
                seed("ln2", b, NB)
                for t in range(NQK):
                    evacuate_qk(b + 1, t)
                modulate(b, 2, h2T, FFN_BANK)
                routing(b)
                run(b + 1, b)
            seed("ln2", B - 1, NB)
            modulate(B - 1, 2, h2T, FFN_BANK)
            routing(B - 1)
            run(None, B - 1)

        @block.vector
        def _(dve):
            def row_stats(tag, b, first, count, mv, rstd):
                v, bits, lg, r0, a, e = [t_[:, 0:count] for t_ in (veps, vbits, logv, rstd0, ra, re)]
                for i in range(count):
                    nc.vector.bn_stats(stats[:, i, :], xs[:, first + i, :]).then_inc(s[f"{tag}_stat"], 1)
                for i in range(count):
                    wait_apart(dve, f"{tag}_stat", b, i + 1)
                    nc.vector.bn_aggr(mv[:, i, :], stats[:, i, :]).then_inc(s[f"{tag}_aggr"], 1)
                wait(dve, f"{tag}_aggr", b, count)
                nc.vector.tensor_scalar(v, mv[:, :, 1], LN_EPS, None, ALU.add).then_inc(s[f"{tag}_veps"], 1)
                wait(dve, f"{tag}_veps", b, 1)
                nc.vector.tensor_copy(bits, v.bitcast(U32)).then_inc(s[f"{tag}_bits"], 1)
                wait(dve, f"{tag}_bits", b, 1)
                nc.vector.tensor_scalar(lg, bits, LN_SLOPE, -LN_AT_ZERO, ALU.mult, ALU.add).then_inc(s[f"{tag}_log"], 1)
                poly = f"{tag}_poly"
                wait(dve, f"{tag}_seed", b, 1)
                nc.vector.tensor_tensor(a, r0, r0, ALU.mult).then_inc(s[poly], 1)
                wait(dve, poly, b, 1)
                nc.vector.tensor_tensor(a, a, v, ALU.mult).then_inc(s[poly], 1)
                wait(dve, poly, b, 2)
                nc.vector.tensor_scalar(e, a, -1.0, 1.0, ALU.mult, ALU.add).then_inc(s[poly], 1)
                wait(dve, poly, b, 3)
                nc.vector.tensor_scalar(a, e, 35 / 128, 5 / 16, ALU.mult, ALU.add).then_inc(s[poly], 1)
                wait(dve, poly, b, 4)
                nc.vector.tensor_tensor(a, a, e, ALU.mult).then_inc(s[poly], 1)
                wait(dve, poly, b, 5)
                nc.vector.scalar_tensor_tensor(out=a, in0=a, scalar=3 / 8, in1=e, op0=ALU.add, op1=ALU.mult).then_inc(s[poly], 1)
                wait(dve, poly, b, 6)
                nc.vector.scalar_tensor_tensor(out=a, in0=a, scalar=1 / 2, in1=e, op0=ALU.add, op1=ALU.mult).then_inc(s[poly], 1)
                wait(dve, poly, b, 7)
                nc.vector.scalar_tensor_tensor(out=rstd[:, 0:count], in0=a, scalar=1.0, in1=r0, op0=ALU.add, op1=ALU.mult).then_inc(s[poly], 1)
                wait(dve, poly, b, 8)

            def normalise(b, n, xhat, mv, rstd):
                for i in range(NB):
                    nc.vector.tensor_scalar(xhat[:, i, :], xs[:, b * NB + i, :], mv[:, i, 0:1], rstd[:, i:i + 1],
                                            ALU.subtract, ALU.mult).then_inc(s[f"ln{n}_xhat"], 1)

            def mod_of(b, n):
                nc.vector.tensor_copy(modc[:, n - 1].rearrange("p a k -> p (a k)"),
                                      mod_t[:, 2 * n - 2:2 * n].rearrange("p a k b -> p (a k) b")[:, :, b]).then_inc(s[f"mod{n}_now"], 1)

            def split_qk(b, t):
                wait(dve, "qk_evac", b, t + 1)
                nc.vector.tensor_copy(qk_p[:, t, 0, :], qk_f[:, t % 2, :]).then_inc(s["qk_hi"], 1)
                wait(dve, "qk_hi", b, t + 1)
                nc.vector.tensor_tensor(qk_r, qk_f[:, t % 2, :], qk_p[:, t, 0, :], ALU.subtract).then_inc(s["qk_res"], 1)
                wait(dve, "qk_res", b, t + 1)
                nc.vector.tensor_copy(qk_p[:, t, 1, :], qk_r).then_inc(s["qk_mid"], 1)
                wait(dve, "qk_mid", b, t + 1)
                nc.vector.tensor_tensor(qk_p[:, t, 2, :], qk_r, qk_p[:, t, 1, :], ALU.subtract).then_inc(s["qk_parts"], 1)

            def evacuate_v(b):
                for i in range(NB):
                    wait(dve, "v_ps", b, i // 2 * 2 + 2)
                    nc.vector.tensor_tensor(V[:, i, :, 0:DH], ps[:, 2 + i // 2, (i % 2) * D:(i % 2 + 1) * D].rearrange("p (h d) -> p h d", h=H),
                                            b_v[:].rearrange("p (h d) -> p h d", h=H), ALU.add).then_inc(s["v_ready"], 1)

            def routing(b):
                wait(dve, "logit_ps", b, 1)
                nc.vector.tensor_copy(logit[:].rearrange("p i e -> p (i e)"), ps[:, 5, 0:NB * E]).then_inc(s["logit_ready"], 1)
                wait_apart(dve, "logit_ready", b, 1)
                for i in range(NB):
                    nc.vector.max(top[:, i, :], logit[:, i, :]).then_inc(s["top_ready"], 1)
                for i in range(NB):
                    wait_apart(dve, "top_ready", b, i + 1)
                    nc.vector.max_index(top_i[:, i, :], top[:, i, :], logit[:, i, :]).then_inc(s["topi_ready"], 1)
                nc.vector.tensor_tensor(rdiff[:], top[:, :, 1], top[:, :, 0], ALU.subtract).then_inc(s["rdiff_ready"], 1)
                wait(dve, "topi_ready", b, NB)
                nc.vector.tensor_copy(top_f[:], top_i[:, :, 0:2]).then_inc(s["topf_ready"], 1)
                wait(dve, "topf_ready", b, 1)
                for k in range(2):
                    for i in range(NB):
                        last = nc.vector.tensor_scalar(pick[:, k, i, :], ecol, top_f[:, i, k:k + 1], LORA_SCALE, ALU.is_equal, ALU.mult)
                    last.then_inc(s["pick_ready"], 1)
                wait(dve, "rexp_ready", b, 1)
                nc.vector.tensor_scalar(rsum[:], rexp[:], 1.0, 2.0, ALU.add, ALU.mult).then_inc(s["rsum_ready"], 1)
                wait(dve, "rsum_ready", b, 1)
                nc.vector.reciprocal(rw[:], rsum[:]).then_inc(s["rw_ready"], 1)
                wait(dve, "rw_ready", b, 1)
                for i in range(NB):
                    last = nc.vector.tensor_scalar(pick[:, 2, i, :], ecol, 0.0, rw[:, i:i + 1], ALU.mult, ALU.add)
                last.then_inc(s["pick_ready"], 1)
                wait(dve, "u_ps", b, 2)
                wait(dve, "pickT_ready", b, 1)
                for k in range(2):
                    nc.vector.tensor_tensor(um[:, k, :], ps[:, 6 + k, :], pickT[:, 0, :], ALU.mult).then_inc(s["um_ready"], 1)
                wait(dve, "pickd_ready", b, 1)
                for k in range(2):
                    nc.vector.tensor_tensor(um[:, 2 + k, :], ps[:, 6 + k, :], pickw[:, 2, :], ALU.mult).then_inc(s["um_ready"], 1)

            def run(ba, bf):
                for _, kind, n in merged("dve", ba is not None, bf is not None):
                    if kind == "p1":
                        at, i, parts = n
                        wait_apart(dve, "p1_ps", ba, i + 1)
                        for h, blk, c in parts:
                            scores = ps[:, at % RING, c:c + WIDTH1[blk]]
                            last = nc.vector.tensor_tensor_reduce(out=scores, in0=scores, in1=qmask[:, S - WIDTH1[blk]:S], scale=-1.0,
                                                                  scalar=3.3e38, op0=ALU.add, op1=ALU.min, accum_out=shift[:, h, blk:blk + 1])
                        last.then_inc(s["p1_max"], 1)
                    elif kind == "norm":
                        z = zsum[:, G * n:G * (n + 1), :].rearrange("p h i -> p (h i)")
                        wait(dve, "p1_done", ba, 2 * UNITS * (n + 1))
                        nc.vector.tensor_copy(zbits[:], z.bitcast(U32)).then_inc(s["zbits_ready"], 1)
                        wait(dve, "zbits_ready", ba, n + 1)
                        nc.vector.tensor_scalar(logz[:], zbits[:], LN_SLOPE, -LN_AT_ZERO, ALU.mult, ALU.add).then_inc(s["log_ready"], 1)
                        wait(dve, "log_ready", ba, n + 1)
                        nc.vector.tensor_tensor(lse[:], shift[:, G * n:G * (n + 1), :].rearrange("p h i -> p (h i)"), logz[:],
                                                ALU.subtract).then_inc(s["lse_first"], 1)
                    elif kind == "norm_t":
                        z = zsum[:, G * n:G * (n + 1), :].rearrange("p h i -> p (h i)")
                        wait(dve, "zinv_ready", ba, n + 1)
                        nc.vector.tensor_tensor(za[:], z, zinv[:], ALU.mult).then_inc(s["log_poly"], 1)
                        wait(dve, "log_poly", ba, 6 * n + 1)
                        nc.vector.tensor_scalar(ze[:], za[:], 1.0, None, ALU.subtract).then_inc(s["log_poly"], 1)
                        wait(dve, "log_poly", ba, 6 * n + 2)
                        nc.vector.tensor_scalar(za[:], ze[:], -1 / 4, 1 / 3, ALU.mult, ALU.add).then_inc(s["log_poly"], 1)
                        wait(dve, "log_poly", ba, 6 * n + 3)
                        nc.vector.tensor_tensor(za[:], za[:], ze[:], ALU.mult).then_inc(s["log_poly"], 1)
                        wait(dve, "log_poly", ba, 6 * n + 4)
                        nc.vector.scalar_tensor_tensor(out=za[:], in0=za[:], scalar=-1 / 2, in1=ze[:], op0=ALU.add, op1=ALU.mult).then_inc(s["log_poly"], 1)
                        wait(dve, "log_poly", ba, 6 * n + 5)
                        nc.vector.scalar_tensor_tensor(out=za[:], in0=za[:], scalar=1.0, in1=ze[:], op0=ALU.add, op1=ALU.mult).then_inc(s["log_poly"], 1)
                        wait(dve, "log_poly", ba, 6 * n + 6)
                        nc.vector.tensor_tensor(lse[:], lse[:], za[:], ALU.subtract).then_inc(s["lse_ready"], 1)
                        wait(dve, "lse_ready", ba, n + 1)
                        nc.vector.tensor_copy(lse_p[:, 0, :], lse[:]).then_inc(s["lse_hi"], 1)
                        wait(dve, "lse_hi", ba, n + 1)
                        nc.vector.tensor_tensor(lse_r[:], lse[:], lse_p[:, 0, :], ALU.subtract).then_inc(s["lse_res"], 1)
                        wait(dve, "lse_res", ba, n + 1)
                        nc.vector.tensor_copy(lse_p[:, 1, :], lse_r[:]).then_inc(s["lse_mid"], 1)
                        wait(dve, "lse_mid", ba, n + 1)
                        nc.vector.tensor_tensor(lse_p[:, 2, :], lse_r[:], lse_p[:, 1, :], ALU.subtract).then_inc(s["lse_parts"], 1)
                    elif kind == "floor":
                        slot = 2 * n % NPROB
                        wait(dve, "p2_exp", ba, UNITS * (n + 1))
                        for h in (slot, slot + 1):
                            last = nc.vector.tensor_scalar(prob[:, h, :], prob[:, h, :], PROB_FLOOR, None, ALU.max)
                        last.then_inc(s["p2_ready"], 1)
                    elif kind == "y":
                        for i in range(NB):
                            wait(dve, "y_ps", ba, i // 2 * 2 + 2)
                            if i >= 1:
                                wait(dve, "x1_ready", ba, i)
                            nc.vector.tensor_tensor(ysb[:], ps[:, 2 + i // 2, (i % 2) * D:(i % 2 + 1) * D], b_o[:], ALU.add).then_inc(s["y_biased"], 1)
                            wait(dve, "y_biased", ba, i + 1)
                            nc.vector.tensor_tensor(ysb[:], ysb[:], gates[:, ba, 0, :], ALU.mult).then_inc(s["y_gated"], 1)
                            wait(dve, "y_gated", ba, i + 1)
                            nc.vector.tensor_tensor(xs[:, ba * NB + i, :], xs[:, ba * NB + i, :], ysb[:], ALU.add).then_inc(s["x1_ready"], 1)
                    elif kind in ("first", "second"):
                        f, cols, bank, turn, m = of_step(n)
                        slot, x_, dst = (0, "fa", act1) if kind == "first" else (1, "fb", act2)
                        m0 = 0 if f < NF else FT
                        wait(dve, x_ + "_tanh", bf, n + 1)
                        nc.vector.scalar_tensor_tensor(out=sil[m0:m0 + m, slot, :], in0=sil[0:m, slot, :], scalar=1.0, in1=ps[0:m, bank, 0:HS],
                                                       op0=ALU.add, op1=ALU.mult).then_inc(s[x_ + "_gate"], 1)
                        wait(dve, x_ + "_gate", bf, n + 1)
                        if n >= 2:
                            wait(dve, "down_ps", bf, n - 1)
                        h3 = ps[:, bank, HS:2 * HS] if f < NF else ps[FT:2 * FT, bank, 0:HS]
                        nc.vector.tensor_tensor(dst[0:m, turn, :], h3, sil[m0:m0 + m, slot, :], ALU.mult).then_inc(s[x_ + "_act"], 1)
                    elif kind == "weigh":
                        cols = slice(n * HS, (n + 1) * HS)
                        wait(dve, "down_ps", bf, NFT * (n + 1))
                        wait(dve, "pickw_ready", bf, 2)
                        if n:
                            wait(dve, "o_ps", bf, 2)
                        nc.vector.tensor_tensor(tm[:, 0, :], ps[:, T_BANK, 0:HS], pickw[:, 0, cols], ALU.mult).then_inc(s["tm_1"], 1)
                        nc.vector.tensor_tensor(tm[:, 1, :], ps[:, T_BANK, HS:2 * HS], pickw[:, 1, cols], ALU.mult).then_inc(s["tm_2"], 1)
                        wait(dve, "tm_2", bf, n + 1)
                        nc.vector.tensor_tensor(tm[:, 0, :], tm[:, 0, :], tm[:, 1, :], ALU.add).then_inc(s["tm_ready"], 1)
                    elif kind == "result":
                        wait(dve, "o_ps", bf, 2 * n + 2)
                        for i in (2 * n, 2 * n + 1):
                            if i >= 1:
                                wait(dve, "o_ready", bf, i)
                            nc.vector.tensor_tensor(osb[:], ps[:, OUT_BANK, (i % 2) * D:(i % 2 + 1) * D], gates[:, bf, 1, :], ALU.mult).then_inc(s["o_gated"], 1)
                            wait(dve, "o_gated", bf, i + 1)
                            nc.vector.tensor_tensor(xs[:, bf * NB + i, :], xs[:, bf * NB + i, :], osb[:], ALU.add).then_inc(s["o_ready"], 1)

            dve.wait_ge(s["small_in"], 80)
            nc.vector.tensor_copy(slope_p[:, 0:1], slope[:]).then_inc(s["sl_1"], 1)
            dve.wait_ge(s["sl_1"], 1)
            nc.vector.tensor_tensor(slope_r[:, 0:1], slope[:], slope_p[:, 0:1], ALU.subtract).then_inc(s["sl_2"], 1)
            dve.wait_ge(s["sl_2"], 1)
            nc.vector.tensor_copy(slope_p[:, 1:2], slope_r[:, 0:1]).then_inc(s["sl_3"], 1)
            dve.wait_ge(s["sl_3"], 1)
            nc.vector.tensor_tensor(slope_p[:, 2:3], slope_r[:, 0:1], slope_p[:, 1:2], ALU.subtract).then_inc(s["sl_4"], 1)
            dve.wait_ge(s["sl_4"], 1)
            dve.wait_ge(s["const_in"], 16)
            for i in range(3):
                for sign in (1.0, -1.0):
                    nc.vector.tensor_scalar(slope_w[:, i if sign > 0 else 3 + i, :], slope_p[:, i:i + 1].to_broadcast([H, S]),
                                            sign, None, ALU.mult).then_inc(s["slope_wide"], 1)
            nc.vector.tensor_scalar(b_qk[:, 0:KT], b_qk[:, 0:KT], SCALE, None, ALU.mult).then_inc(s["bq_scaled"], 1)
            nc.vector.tensor_copy(ident_b[:], ident).then_inc(s["const_ready"], 1)
            nc.vector.tensor_copy(kmask_b[:], kmask).then_inc(s["const_ready"], 1)
            dve.wait_ge(s["x_in"], 32)
            dve.wait_ge(s["zero_done"], 6)
            dve.wait_ge(s["const_ready"], 2)
            dve.wait_ge(s["bq_scaled"], 1)
            row_stats("ln1a", 0, 0, NB, mv1[:, 0:NB], rstd1[:, 0:NB])
            normalise(0, 1, xhat1, mv1, rstd1)
            dve.wait_ge(s["cs_ready"], 1)
            nc.vector.tensor_copy(c_wide, c_silu[:].rearrange("p k (b o) -> p k b o", o=1).to_broadcast([P, KT, B, P])).then_inc(s["cwide_ready"], 1)
            dve.wait_ge(s["mod_ps"], 1)
            mods = ps[:, 4, 0:4 * KT * B].rearrange("p (a k b) -> p a k b", a=4, k=KT)
            for a in range(4):
                nc.vector.tensor_scalar(mod_t[:, a], mods[:, a], float(a % 2), None, ALU.add).then_inc(s["modt_ready"], 1)
            dve.wait_ge(s["modt_ready"], 4)
            mod_of(0, 1)
            for t in range(NQK):
                split_qk(0, t)
            evacuate_v(0)
            for b in range(B):
                dve.wait_ge(s["gate_ps"], b + 1)
                if b:
                    dve.wait_ge(s["gates_ready"], b)
                g = ps[:, 6 + b % 2, :]
                nc.vector.tensor_scalar(g_abs, g, -1.0, None, ALU.mult).then_inc(s["gate_neg"], 1)
                dve.wait_ge(s["gate_neg"], b + 1)
                nc.vector.tensor_tensor(g_abs, g, g_abs, ALU.max).then_inc(s["gate_abs"], 1)
                nc.vector.tensor_scalar(g_sgn, g, 0.0, 2.0, ALU.is_ge, ALU.mult).then_inc(s["gate_sgn"], 1)
                dve.wait_ge(s["gate_sgn"], b + 1)
                nc.vector.tensor_scalar(g_abs, g_abs, GATE_FLOOR, None, ALU.max).then_inc(s["gate_floor"], 1)
                dve.wait_ge(s["gate_floor"], b + 1)
                nc.vector.scalar_tensor_tensor(out=gates[:, b].rearrange("p a d -> p (a d)"), in0=g_sgn, scalar=-1.0, in1=g_abs,
                                               op0=ALU.add, op1=ALU.mult).then_inc(s["gates_ready"], 1)
            row_stats("ln1b", 0, NB, (B - 1) * NB, mv1[:, NB:], rstd1[:, NB:])
            dve.wait_ge(s["gates_ready"], B)
            run(0, None)
            with dve.Fori(0, B - 1) as b:
                nc.vector.tensor_copy(mv_now[:], mv1[:, bass.ds((b + 1) * NB, NB), 0:1]).then_inc(s["ln1_now"], 1)
                nc.vector.tensor_copy(rstd_now[:], rstd1[:, bass.ds((b + 1) * NB, NB)]).then_inc(s["ln1_now"], 1)
                mod_of(b + 1, 1)
                wait(dve, "ln1_now", b, 2)
                normalise(b + 1, 1, xhat1, mv_now, rstd_now)
                row_stats("ln2", b, b * NB, NB, mv2, rstd2)
                normalise(b, 2, xhat2, mv2, rstd2)
                mod_of(b, 2)
                for t in range(NQK):
                    split_qk(b + 1, t)
                evacuate_v(b + 1)
                routing(b)
                run(b + 1, b)
            wait_apart(dve, "x1_ready", B - 1, NB)
            row_stats("ln2", B - 1, (B - 1) * NB, NB, mv2, rstd2)
            normalise(B - 1, 2, xhat2, mv2, rstd2)
            mod_of(B - 1, 2)
            routing(B - 1)
            run(None, B - 1)

        @block.tensor
        def _(pe):
            mm = nc.tensor.matmul

            def transposes(b, n, xhat, bank):
                for k in range(KT):
                    for i in range(NB):
                        wait(pe, f"ln{n}_xhat", b, i + 1)
                        last = nc.tensor.transpose(ps[:, bank + k, i * P:(i + 1) * P], xhat[:, i, k * P:(k + 1) * P], ident)
                    last.then_inc(s[f"h{n}T_ps"], 1)

            def front(b):
                transposes(b, 1, xhat1, 0)
                wait(pe, "h1T_ready", b, KT)
                for t in range(NQK):
                    for k in range(KT):
                        last = mm(ps[:, (t + 2) % 4, :], wqkv[:, k, t * P:(t + 1) * P], hT[:, k, :], start=k == 0, stop=k == KT - 1)
                    last.then_inc(s["qk_ps"], 1)
                wait(pe, "qk_evac", b, 2)
                for i in range(NB):
                    for k in range(KT):
                        last = mm(ps[:, 2 + i // 2, (i % 2) * D:(i % 2 + 1) * D], hT[:, k, i * P:(i + 1) * P],
                                  wqkv[:, k, 2 * D:3 * D], start=k == 0, stop=k == KT - 1)
                    last.then_inc(s["v_ps"], 1)

            def targets(n):
                f, _, bank, _, _ = of_step(n)
                c0, _ = tile_cols(f)
                return [(ps[:, bank, 0:HS], c0), (ps[:, bank, HS:2 * HS], c0 + P)][:2 if f < NF else 1]

            def base(b, n):
                f, cols, bank, _, _ = of_step(n)
                if n == 1:
                    wait(pe, "pickT_ready", b, 4)
                if n >= 2:
                    wait(pe, "fb_act", b, n - 1)
                for j, (dst, c0) in enumerate(targets(n)):
                    for k in range(KT):
                        mm(dst, w13[:, k, c0:c0 + P], h2T[:, k, cols], start=j == 0 and k == 0, stop=True, skip_group_check=True)

            def lora(b, n, slot):
                f, cols, bank, _, _ = of_step(n)
                if n == 0:
                    wait(pe, "um_ready", b, 2 + 2 * slot)
                if slot == 1:
                    wait(pe, "fa_act", b, n + 1)
                for j, (dst, c0) in enumerate(targets(n)):
                    if f < NF:
                        last = mm(dst, b13[:, c0:c0 + P], um[:, 2 * slot + j, cols], start=False, stop=True, skip_group_check=True)
                    else:
                        for q in range(2):
                            last = mm(dst[q * FT:(q + 1) * FT], b13[:, c0 + q * FT:c0 + (q + 1) * FT], um[:, 2 * slot + q, cols],
                                      start=False, stop=True, skip_group_check=True)
                last.then_inc(s["fb_ps" if slot else "fa_ps"], 1)

            def ffn_front(b):
                transposes(b, 2, xhat2, FFN_BANK)
                wait(pe, "h2T_ready", b, KT)
                for i in range(NB):
                    for k in range(KT):
                        last = mm(ps[:, 5, i * E:(i + 1) * E], h2T[:, k, i * P:(i + 1) * P], gate_w[:, k, :], start=k == 0, stop=k == KT - 1)
                last.then_inc(s["logit_ps"], 1)
                for t in range(2):
                    for k in range(KT):
                        last = mm(ps[:, 6 + t, :], a13[:, k, t * P:(t + 1) * P], h2T[:, k, :], start=k == 0, stop=k == KT - 1)
                    last.then_inc(s["u_ps"], 1)
                base(b, 0)
                for k in range(3):
                    bank = (5, 3, 5)[k]
                    wait(pe, "pick_ready", b, k + 1)
                    if k == 2:
                        wait(pe, "pickT_ready", b, 1)
                    for i in range(NB):
                        last = nc.tensor.transpose(ps[:, bank, i * P:(i + 1) * P], pick[:, k, i, :], ident)
                    last.then_inc(s["pick_ps"], 1)

            def run(ba, bf):
                norms, sums = 0, 0
                for _, kind, n in merged("pe", ba is not None, bf is not None):
                    if kind in ("p1", "p2"):
                        at, i, parts = n
                        if at == 0:
                            wait(pe, "rows_landed", ba, per["rows_landed"])
                            wait(pe, "v_ready", ba, NB)
                            wait(pe, "qk_evac", ba, NQK)
                        if at >= RING:
                            was, j, _ = units[at - RING]
                            wait(pe, "p1_done" if was == "p1" else "p2_exp", ba, j + 1)
                    if kind == "p1":
                        for h, blk, c in parts:
                            last = mm(ps[:, at % RING, c:c + WIDTH1[blk]], QA[0:R_NORM, h, blk * P:(blk + 1) * P],
                                      KA[0:R_NORM, h, 0:WIDTH1[blk]], start=True, stop=True)
                        last.then_inc(s["p1_ps"], 1)
                    elif kind == "p2":
                        if i % (2 * UNITS) == 0:
                            wait(pe, "lse_landed", ba, 48 * (i // (2 * UNITS) + 1))
                        for h, blk, c in parts:
                            mm(ps[:, at % RING, c:c + P], ident_b[:], kmask_b[:], start=True, stop=True)
                            last = mm(ps[:, at % RING, c:c + WIDTH2[blk]], KA[0:R_ALL, h, blk * P:(blk + 1) * P], QA[0:R_ALL, h, blk * P:S],
                                      start=False, stop=True, skip_group_check=True)
                        last.then_inc(s["p2_ps"], 1)
                    elif kind == "norm_t":
                        wait_apart(pe, "lse_parts", ba, n + 1)
                        if norms:
                            wait(pe, "lse_evac", ba, norms)
                        if sums:
                            wait(pe, "att_ready", ba, sums)
                        norms += 1
                        nc.tensor.transpose(ps[:, ATT_BANK, :].bitcast(BF16)[0:3 * G * NB, 0:P], lse_p[:].rearrange("p c n -> p (c n)"),
                                            ident_b[:]).then_inc(s["lse_ps"], 1)
                    elif kind == "pv":
                        wait(pe, "p2_ready", ba, 2 * (n + 1))
                        wait(pe, "lse_evac", ba, norms)
                        if sums:
                            wait(pe, "att_ready", ba, sums)
                        else:
                            wait(pe, "vsuf_ready", ba, 1)
                        sums += 1
                        for i in range(NB - 1):
                            for c in range(G):
                                hh = G * n + c
                                v = V[:, 3, hh, :] if i == 2 else Vsuf[:, i, hh, :]
                                mm(ps[32 * c:32 * c + 32, ATT_BANK, i * P:(i + 1) * P], v, floor_c[:], start=i == 0, stop=True,
                                   skip_group_check=True)
                        for j in (3, 2, 1, 0):
                            for c in range(G):
                                hh = G * n + c
                                last = mm(ps[32 * c:32 * c + 32, ATT_BANK, j * P:S], V[:, j, hh, :],
                                          prob[:, hh % NPROB, START2[j]:START2[j] + WIDTH2[j]], start=False, stop=True,
                                          skip_group_check=True)
                        last.then_inc(s["pv_ps"], 1)
                    elif kind == "y":
                        wait(pe, "att_ready", ba, NG)
                        wait(pe, "p2_exp", ba, UNITS * PAIRS)
                        for i in range(NB):
                            for g in range(NG):
                                last = mm(ps[:, 2 + i // 2, (i % 2) * D:(i % 2 + 1) * D], att[:, g, i * P:(i + 1) * P], wo[:, g, :],
                                          start=g == 0, stop=g == NG - 1)
                            last.then_inc(s["y_ps"], 1)
                    elif kind == "base":
                        if n:
                            base(bf, n)
                    elif kind == "first":
                        lora(bf, n, 0)
                    elif kind == "second":
                        lora(bf, n, 1)
                    elif kind == "down":
                        f, cols, _, turn, _ = of_step(n)
                        wait(pe, "gsum_ready", bf, n + 1)
                        if n == NFT:
                            wait(pe, "tm_2", bf, 1)
                            wait(pe, "o_gated", bf, 2)
                        mm(ps[:, T_BANK, 0:HS], a2[:, f, :], act1[:, turn, :], start=f == 0, stop=True, skip_group_check=True)
                        mm(ps[:, T_BANK, HS:2 * HS], a2[:, f, :], act2[:, turn, :], start=False, stop=True, skip_group_check=True)
                        for i in range(2):
                            last = mm(ps[:, OUT_BANK, i * D:(i + 1) * D], gsum[:, turn, i * P:(i + 1) * P], w2[:, f, :],
                                      start=f == 0 and i == 0, stop=True, skip_group_check=True)
                        last.then_inc(s["down_ps"], 1)
                    elif kind == "result":
                        wait(pe, "tm_ready", bf, n + 1)
                        for i in range(2):
                            mm(ps[:, OUT_BANK, i * D:(i + 1) * D], tm[:, 0, i * P:(i + 1) * P], b2[:], start=False, stop=True,
                               skip_group_check=True).then_inc(s["o_ps"], 1)

            pe.wait_ge(s["const_ready"], 2)
            pe.wait_ge(s["wmod_in"], 16)
            pe.wait_ge(s["cs_ready"], 1)
            for a, chunk in enumerate((0, 1, 3, 4)):
                for t in range(KT):
                    for k in range(KT):
                        last = mm(ps[:, 4, (a * KT + t) * B:(a * KT + t + 1) * B], wmod_s[:, k, chunk * D + t * P:chunk * D + (t + 1) * P],
                                  c_silu[:, k, :], start=k == 0, stop=k == KT - 1)
            last.then_inc(s["mod_ps"], 1)
            pe.wait_ge(s["wqkv_in"], 16)
            front(0)
            pe.wait_ge(s["cwide_ready"], 1)
            for b in range(B):
                if b >= 2:
                    pe.wait_ge(s["gates_ready"], b - 1)
                for n, chunk in enumerate((2, 5)):
                    for k in range(KT):
                        last = mm(ps[:, 6 + b % 2, n * D:(n + 1) * D], c_wide[:, k, b, :], wmod_s[:, k, chunk * D:(chunk + 1) * D],
                                  start=k == 0, stop=k == KT - 1)
                last.then_inc(s["gate_ps"], 1)
            pe.wait_ge(s["rows_in"], 16 * 15)
            pe.wait_ge(s["out_w_in"], 64)
            pe.wait_ge(s["ffn_in"], 128)
            pe.wait_ge(s["small_in"], 80)
            pe.wait_ge(s["gates_ready"], B)
            run(0, None)
            with pe.Fori(0, B - 1) as b:
                wait(pe, "y_biased", b, NB)
                front(b + 1)
                ffn_front(b)
                run(b + 1, b)
            wait(pe, "x1_ready", B - 1, NB)
            ffn_front(B - 1)
            run(None, B - 1)


_OUT = (4, 512, 256)


def kernel(L0_attn_qkv, L0_attn_in_proj, L0_attn_in_proj_bias, L0_attn_out_w, L0_attn_out_b, L0_attn_alibi_slopes, L0_ffn_gate_w,
           L0_ffn_w1, L0_ffn_w3, L0_ffn_w2, L0_ffn_a1, L0_ffn_b1, L0_ffn_a3, L0_ffn_b3, L0_ffn_a2, L0_ffn_b2, L0_c, L0_wmod):
    import numpy as np
    import ml_dtypes
    import concourse.bacc as bacc
    from concourse.bass_utils import run_bass_kernel_spmd

    a = {k: np.asarray(v) for k, v in dict(
        x=L0_attn_qkv, in_proj=L0_attn_in_proj, bqkv=L0_attn_in_proj_bias, out_w=L0_attn_out_w, bo=L0_attn_out_b,
        slopes=L0_attn_alibi_slopes, gate=L0_ffn_gate_w, w1=L0_ffn_w1, w3=L0_ffn_w3, w2=L0_ffn_w2, a1=L0_ffn_a1, b1=L0_ffn_b1,
        a3=L0_ffn_a3, b3=L0_ffn_b3, a2=L0_ffn_a2, b2=L0_ffn_b2, c=L0_c, wmod=L0_wmod).items()}
    E, R, D = a["a1"].shape
    F = a["w1"].shape[0]

    def pair(u, v):
        cuts = list(range(0, F, 128))
        return np.concatenate([m[:, n:n + 128] for n in cuts for m in (u, v)], axis=1)

    def ranks(w):
        return w.transpose(0, 2, 1).reshape(E * R, w.shape[1])

    n = np.arange(128)
    consts = np.zeros((128, 896), np.float32)
    consts[:, 0:128] = np.eye(128)
    consts[:, 128 + 384:640] = np.where(n[None, :] > n[:, None], MASKED, 0.0)
    consts[:, 640:768] = np.where(n[:, None] > n[None, :], MASKED, 0.0)
    consts[:, 768:896] = n[None, :] // R
    pos = np.ones((2, 1, 16, 512), np.float32)
    pos[0] = np.arange(512) - 256
    arrays = dict(
        x=a["x"], wqkvT=a["in_proj"].T, bqk=a["bqkv"][:2 * D].reshape(-1, 128).T, bv=a["bqkv"][2 * D:], woT=a["out_w"].T, bo=a["bo"], slopes=a["slopes"], gateT=a["gate"].T,
        w13T=pair(a["w1"].T, a["w3"].T), w2T=a["w2"].T, a13T=np.concatenate([a["a1"].reshape(E * R, D).T, a["a3"].reshape(E * R, D).T], axis=1),
        b13T=pair(ranks(a["b1"]), ranks(a["b3"])), a2T=a["a2"].reshape(E * R, F).T, b2T=ranks(a["b2"]), cT=a["c"].T, wmod=a["wmod"],
        consts=consts, pos_rows=pos.astype(ml_dtypes.bfloat16))
    nc = bacc.Bacc("TRN2", target_bir_lowering=False, num_devices=1)
    feed, args = {}, []
    for name, v in arrays.items():
        v = np.ascontiguousarray(v)
        feed[f"in_{name}"] = v
        args.append(nc.dram_tensor(f"in_{name}", v.shape, mybir.dt.from_np(v.dtype), kind="ExternalInput").ap())
    args.append(nc.dram_tensor("result", _OUT, F32, kind="ExternalOutput").ap())
    adaln_block(nc, *args)
    return run_bass_kernel_spmd(nc, [feed], core_ids=[0]).results[0]["result"]
```

```python
from contextlib import ExitStack

import concourse.bass as bass
from concourse import mybir

P = 128
ALU = mybir.AluOpType
ACT = mybir.ActivationFunctionType
BF16 = mybir.dt.bfloat16
F32 = mybir.dt.float32
U32 = mybir.dt.uint32

LN_EPS = 1e-5
GATE_FLOOR = 0.25
PROB_FLOOR = 1e-10
LORA_SCALE = 2.0
MASKED = -3e38
LN_SLOPE = 0.6931471805599453 / 2 ** 23
LN_AT_ZERO = (127 - 0.043) * 0.6931471805599453


def adaln_block(nc, x, wqkvT, bqk, bv, woT, bo, slopes, gateT, w13T, w2T, a13T, b13T, a2T, b2T, cT, wmod,
                consts, pos_rows, out):
    B, S, D = x.shape
    H = slopes.shape[0]
    DH = D // H
    F = w2T.shape[0]
    E = gateT.shape[1]
    KT = D // P
    NB = S // P
    G = 4
    NG = H // G
    NF = F // P
    FT = F - NF * P
    NFT = NF + 1
    NQK = 2 * KT
    SCALE = float(DH) ** -0.5
    assert (B, S, D, H, F, E) == (4, 512, 256, 16, 704, 8) and FT == 64 and b13T.shape[0] == P

    R_SLOPE = 6 * DH
    R_POS = R_SLOPE + 3
    R_NORM = R_SLOPE + 6
    R_ALL = R_SLOPE + 9
    Q_PART = (0, 0, 1, 0, 1, 2)
    K_PART = (0, 1, 0, 2, 1, 0)

    WIDTH1, WIDTH2 = (128, 256, 384, 512), (512, 384, 256, 128)
    START2 = (0, 512, 1024, 896)
    COLS = 1280

    def pair_units(kind, p):
        h = 2 * p
        if kind == "p1":
            return [[(h, 3, 0)], [(h, 2, 0), (h, 0, 384)], [(h + 1, 3, 0)], [(h + 1, 2, 0), (h + 1, 0, 384)], [(h, 1, 0), (h + 1, 1, 256)]]
        return [[(h, 2, 0), (h + 1, 2, 256)], [(h, 0, 0)], [(h, 1, 0), (h, 3, 384)], [(h + 1, 0, 0)], [(h + 1, 1, 0), (h + 1, 3, 384)]]

    PAIRS, LEAD = H // 2, 4
    UNITS = 5
    LSE_AFTER = 6
    units = []
    for p in range(PAIRS + LEAD):
        p2 = [("p2", (p - LEAD) * UNITS + i, u) for i, u in enumerate(pair_units("p2", p - LEAD))] if p >= LEAD else []
        p1 = [("p1", p * UNITS + i, u) for i, u in enumerate(pair_units("p1", p))] if p < PAIRS else []
        if p1 and p2:
            units += [u for both in zip(p2, p1) for u in both]
        else:
            units += p1 + p2
    for g in range(NG):
        end = [(kind, i) for kind, i, _ in units].index(("p1", 2 * UNITS * (g + 1) - 1))
        units.insert(end + 1 + LSE_AFTER, ("lse", g, None))
    place = {(kind, i): n for n, (kind, i, _) in enumerate(units)}
    NS = 2 * NFT
    HS = S // 2

    ALONE = dict(act_p1=2.1, act_p2=1.85, dve_p1=0.8, floor=4.1, pv=5.8, pv_pace=0.4, act_pv=1.8, log=2.2, y=1.1,
                 base=0, step=2.0, pace=0.08, slot2=2.1, down=4.45, after_1=0.55, after_2=0.2, weigh=0.15, result=0.7)
    BESIDE = dict(act_p1=0.95, act_p2=1.9, dve_p1=0.0, floor=1.75, pv=3.75, pv_pace=0.0, act_pv=1.95, log=1.35, y=1.25, base=1.1,
                  step=7.9, pace=1.2, slot2=5.1, down=12.3, after_1=0.5, after_2=1.5, weigh=1.3, result=3.25, base_0=-10.3, base_1=-6.7)

    def attention_steps(engine, alone, more):
        at = ALONE if alone else BESIDE
        late = {"act": {"p1": at["act_p1"], "p2": at["act_p2"]}, "dve": {"p1": at["dve_p1"]}}.get(engine, {})
        end = len(units) + at["pv"] + at["y"]
        steps = [(end, "y", 0)]
        if more and engine in ("pe", "act", "dve"):
            steps.append((end + {"dve": -1.7, "pe": 0.1, "act": max(0.1, at["act_pv"] - 2.0)}[engine], "next", 0))
        if alone and engine in ("pe", "act"):
            steps += [(20 + 4 * b + (1.5 if engine == "act" else 0), "gates", b) for b in range(B)]
        if alone and engine in ("act", "dve"):
            steps += [(60 + 6 * b + (0.9 if engine == "act" else 0), "statistics", b) for b in range(1, B)]
        for n, (kind, i, parts) in enumerate(units):
            if kind == "lse" and engine != "dve":
                steps.append((n + {"pe": 0, "act": 0.6, "sp": 0.7, "pool": -LSE_AFTER + at["log"] + 0.5}[engine], kind, (n, i, parts)))
            elif engine in ("pe", "act") or kind == "p1" and engine == "dve":
                steps.append((n + late.get(kind, 0), kind, (n, i, parts)))
        for p in range(PAIRS):
            end1, end2 = place["p1", UNITS * p + 4], place["p2", UNITS * p + 4]
            if engine == "dve":
                steps.append((place["p2", UNITS * p + 2] + at["floor"], "floor", 2 * p))
                steps.append((end2 + at["floor"], "floor", 2 * p + 1))
            if p % 2:
                g = p // 2
                if engine in ("act", "pool"):
                    steps.append((end1 + at["log"] + (0.1 if engine == "act" else 0), "norm", g))
                if engine == "pe":
                    steps += [(end2 + at["pv"] + at["pv_pace"] * j, "pv", (g, j)) for j in range(NB)]
                elif engine == "act":
                    steps.append((end2 + at["pv"] + at["act_pv"], "pv", g))
        return steps

    def ffn_steps(engine, alone):
        at = ALONE if alone else BESIDE
        steps = []
        for n in range(NS):
            base = at["base"] + at["step"] * n
            if not alone:
                base = at[f"base_{n}"] if n < 2 else base - 2 * at["step"]
            second, down, pace = base + at["slot2"], base + at["down"], at["pace"]
            if engine == "pe":
                steps += [(base, "base", (n, 0)), (base + pace, "base", (n, 1)), (base + 2 * pace, "first", n), (second, "second", n),
                          (down, "down_t", n), (down + pace, "down_o", n)]
            else:
                steps += [(base + 2 * pace + at["after_1"] + (0.3 if engine == "pool" else 0), "first", n), (second + at["after_2"], "second", n)]
            if n % NFT == NFT - 1:
                steps.append((down + at["weigh"], "weigh", n // NFT))
                steps.append((down + at["result"], "result", n // NFT))
        return steps

    def merged(engine, attention, ffn, more=False):
        return sorted((attention_steps(engine, not ffn, more) if attention else []) + (ffn_steps(engine, not attention) if ffn else []),
                      key=lambda step: step[0])

    def ring(ffn):
        return (0, 1, 2) if ffn else (0, 1, 2, 4, 5)

    with ExitStack() as ctx:
        def sb(name, shape, dt=F32):
            return ctx.enter_context(nc.sbuf_tensor(name, shape, dt))

        ps = ctx.enter_context(nc.psum_tensor("ps", [P, 8, 512], F32))
        ATT_BANK, FFN_BANK, T_BANK, OUT_BANK = 3, 4, 6, 7
        scratch = nc.dram_tensor("qk_scratch", (NQK * P, 3, S), BF16, kind="Internal").ap()

        const = sb("const", [P, 896])
        ident, qmask, kmask, ecol = const[:, 0:128], const[:, 128:640], const[:, 640:768], const[:, 768:896]
        ident_b, kmask_b = sb("ident_b", [P, P], BF16), sb("kmask_b", [P, P], BF16)
        floor_c, half_c = sb("floor_c", [P, P]), sb("half_c", [P, 1])
        wqkv = sb("wqkv", [P, KT, 3 * D])
        wo = sb("wo", [P, NG // 2, D])
        w13 = sb("w13", [P, KT, 2 * F])
        b13 = sb("b13", [P, 2 * F])
        a13 = sb("a13", [P, KT, 2 * P])
        w2, a2, b2 = sb("w2", [P, NFT, D]), sb("a2", [P, NFT, P]), sb("b2", [P, D])
        gate_w = sb("gate_w", [P, KT, E])
        b_qk, b_v, b_o = sb("b_qk", [P, NQK]), sb("b_v", [P, D]), sb("b_o", [P, D])
        c_t, c_silu = sb("c_t", [P, KT, B]), sb("c_silu", [P, KT, B])
        mod_t = sb("mod_t", [P, 4, KT, B])
        gates = sb("gates", [P, B, 2, D])
        slope, slope_r = sb("slope", [H, 1]), sb("slope_r", [H, 2])
        slope_p = sb("slope_p", [H, 3], BF16)

        xs = sb("xs", [P, B * NB, D])
        stats = sb("stats", [P, NB, 6])
        mv1, rstd1 = sb("mv1", [P, B * NB, 2]), sb("rstd1", [P, B * NB])
        mv2, rstd2 = sb("mv2", [P, NB, 2]), sb("rstd2", [P, NB])
        veps, vbits, logv, rstd0, ra, re = [sb(n, [P, NB]) for n in ("veps", "vbits", "logv", "rstd0", "ra", "re")]
        mv_now, rstd_now = sb("mv_now", [P, NB, 1]), sb("rstd_now", [P, NB])
        xhat = sb("xhat", [P, NB, D])
        modc = sb("modc", [P, 2, 2, KT])
        hT, h2T = sb("hT", [P, KT, S]), sb("h2T", [P, KT, S])
        QA, KA = sb("QA", [P, H, S], BF16), sb("KA", [P, H, S], BF16)
        V, Vsuf = sb("V", [P, NB, H, 32]), sb("Vsuf", [P, 2, H, 32])
        shift, zsum = sb("shift", [P, H, NB]), sb("zsum", [P, H, NB])
        zbits, logz, zinv = sb("zbits", [P, G * NB]), sb("logz", [P, G * NB]), sb("zinv", [P, G * NB])
        za, ze = sb("za", [P, G * NB]), sb("ze", [P, G * NB])
        lse, lse_r = sb("lse", [P, G * NB]), sb("lse_r", [P, G * NB])
        lse_p, lse_t = sb("lse_p", [P, 3, G * NB], BF16), sb("lse_t", [3 * G * NB, P], BF16)
        NPROB = 8
        prob = sb("prob", [P, NPROB, COLS])
        att = sb("att", [P, NG // 2, S])
        gbias = xhat[:, 0, :]
        ysb = sb("ysb", [P, 2, D])
        osb = ysb
        early = prob[:].rearrange("p g n -> p (g n)")
        qk_p = early[:, 0:NQK * 3 * S // 2].bitcast(BF16).rearrange("p (t c n) -> p t c n", t=NQK, c=3)
        qk_f = early[:, 3072:3072 + 2 * S].rearrange("p (t n) -> p t n", t=2)
        qk_r = early[:, 4096:4096 + S]
        pick = early[:, 4608:4608 + 3 * S].rearrange("p (k i n) -> p k i n", k=3, i=NB)
        slope_w = early[0:H, 6144:7680].bitcast(BF16).rearrange("p (k n) -> p k n", k=6)

        logit, top, top_i = sb("logit", [P, NB, E]), sb("top", [P, NB, 8]), sb("top_i", [P, NB, 8], U32)
        top_f = sb("top_f", [P, NB, 2])
        rdiff, rexp, rsum, rw = sb("rdiff", [P, NB]), sb("rexp", [P, NB]), sb("rsum", [P, NB]), sb("rw", [P, NB])
        route = sb("route", [P, 11 * S])
        pickT = route[:, 0:4 * S].rearrange("p (k n) -> p k n", k=4)
        pickw = route[:, 4 * S:7 * S].rearrange("p (k n) -> p k n", k=3)
        um = route[:, 7 * S:11 * S].rearrange("p (k n) -> p k n", k=4)
        wmod_s = route[:, 0:KT * 6 * D].rearrange("p (k n) -> p k n", k=KT)
        select = route[0:B, 3072:3072 + B * P].rearrange("p (b n) -> p b n", b=B)
        g_abs, g_sgn, g_all = [route[0:B, c:c + 2 * D] for c in (3584, 4096, 4608)]
        sil, gw, tm = sb("sil", [P, 2, HS]), sb("gw", [P, 2, HS]), sb("tm", [P, 2, HS])
        act1, act2, gsum = sb("act1", [P, 2, HS]), sb("act2", [P, 2, HS]), sb("gsum", [P, 2, HS])

        per = dict(
            gbias_ready=1, x_biased=NB,
            ln1_now=2, ln1_xhat=NB, h1T_ps=KT, h1T_ready=KT,
            ln2_stat=NB, ln2_aggr=NB, ln2_veps=1, ln2_bits=1, ln2_log=1, ln2_seed=1, ln2_poly=8, ln2_xhat=NB, h2T_ps=KT, h2T_ready=KT,
            mod1_now=1, mod2_now=1, qk_ps=NQK, qk_evac=NQK, qk_hi=NQK, qk_res=NQK, qk_mid=NQK, qk_parts=NQK, v_ps=NB, v_ready=2 * NB,
            vsuf_mid=1, vsuf_ready=1, parts_a_out=32, parts_b_out=32, rows_a_landed=16 * 12, rows_b_landed=16 * 12,
            p1_ps=UNITS * PAIRS, p1_max=UNITS * PAIRS, p1_done=UNITS * PAIRS, zbits_ready=NG, log_ready=NG, lse_first=NG, zinv_ready=NG,
            log_poly=8 * NG, lse_ready=NG, lse_hi=NG, lse_res=NG, lse_mid=NG, lse_parts=NG,
            lse_ps=NG, lse_evac=NG, lse_landed=48 * NG, p2_ps=UNITS * PAIRS, p2_exp=UNITS * PAIRS, p2_ready=H, pv_ps=NG, att_ready=NG // 2,
            y_ps=NB, y_gated=NB, x1_ready=NB,
            logit_ps=1, logit_ready=1, top_ready=NB, topi_ready=NB, topf_ready=1, rdiff_ready=1, rexp_ready=1,
            rsum_ready=1, rw_ready=1, pick_ready=3, pick_ps=3, pickT_ready=4, pickd_ready=1, pickw_ready=2, u_ps=2, um_ready=4,
            fa_ps=NS, fa_tanh=NS, fa_gate=NS, fa_act=NS, fb_ps=NS, fb_tanh=NS, fb_gate=NS, fb_act=NS, gw_ready=2 * NS, gsum_ready=NS,
            down_ps=NS, tm_1=2, tm_2=2, tm_ready=2, o_ps=NB, o_gated=NB, o_ready=NB, store_done=16 * NB)
        per.update(ln1_stat=NB, ln1_aggr=NB, ln1_veps=1, ln1_bits=1, ln1_log=1, ln1_seed=1, ln1_poly=8)
        once = """const_in x_in x_rest_in c_in wmod_in wmod_rest_in wqkv_in small_in rows_in out_w_in zero_done ffn_in cs_ready select_ready
            mod_ps modt_ready gate_ps gate_abs gate_sgn gate_neg gate_floor gate_rows gate_wide gates_ready sl_1 sl_2 sl_3 sl_4
            slope_wide bq_scaled const_ready""".split()
        s = {n: ctx.enter_context(nc.semaphore(n)) for n in [*per, *once]}
        block = ctx.enter_context(nc.Block())
        QK_ORDER = (0, 2, 1, 3)

        def wait(eng, name, b, k):
            eng.wait_ge(s[name], b * per[name] + k)

        def wait_apart(eng, name, b, k):
            if isinstance(b, int):
                return wait(eng, name, b, k)
            value = eng.to_reg(b * per[name] + k)
            eng.wait_ge(s["const_ready"], 2)
            eng.wait_ge(s[name], value)

        def tile_cols(f):
            return (f * 2 * P, P) if f < NF else (NF * 2 * P, FT)

        def of_step(n):
            f, half = n % NFT, n // NFT
            return f, slice(half * HS, (half + 1) * HS), FFN_BANK + n % 2, n % 2, P if f < NF else FT

        @block.sync
        def _(sp):
            def load(dst, src, name):
                sp.dma_start(dst, src).then_inc(s[name], 16)

            xv = x.rearrange("b (i p) d -> p (b i) d", p=P)
            load(xs[:, 0:NB, :], xv[:, 0:NB, :], "x_in")
            load(c_t[:], cT.rearrange("(k p) b -> p k b", p=P), "c_in")
            load(const[:], consts, "const_in")
            load(wqkv[:], wqkvT.rearrange("(k p) n -> p k n", p=P), "wqkv_in")
            load(b_qk[:], bqk, "small_in")
            load(b_v[:], bv.rearrange("(o d) -> o d", o=1).to_broadcast([P, D]), "small_in")
            load(b_o[:], bo.rearrange("(o d) -> o d", o=1).to_broadcast([P, D]), "small_in")
            load(slope[:], slopes.rearrange("(h o) -> h o", o=1), "small_in")
            load(gate_w[:], gateT.rearrange("(k p) e -> p k e", p=P), "small_in")
            for i in range(3):
                load(QA[R_POS + i:R_POS + i + 1, :, :], pos_rows[0], "rows_in")
                load(KA[R_SLOPE + i:R_SLOPE + i + 1, :, :], pos_rows[0], "rows_in")
                load(KA[R_NORM + i:R_NORM + i + 1, :, :], pos_rows[1], "rows_in")
            sp.wait_ge(s["slope_wide"], 6)
            for i in range(3):
                load(QA[R_SLOPE + i:R_SLOPE + i + 1, :, :], slope_w[:, i, :], "rows_in")
                load(KA[R_POS + i:R_POS + i + 1, :, :], slope_w[:, 3 + i, :], "rows_in")

            def regroup(b):
                for half, written, landed in ((0, "parts_a_out", "rows_a_landed"), (1, "parts_b_out", "rows_b_landed")):
                    wait(sp, "qk_parts", b, 2 * half + 2)
                    for side in range(2):
                        t = side * KT + half
                        sp.dma_start(scratch[t * P:(t + 1) * P], qk_p[:, t, :, :]).then_inc(s[written], 16)
                    wait(sp, written, b, 32)
                    heads = slice(half * H // 2, (half + 1) * H // 2)
                    for side, dst, parts in ((0, QA, Q_PART), (1, KA, K_PART)):
                        t = side * KT + half
                        src = scratch[t * P:(t + 1) * P].rearrange("(h d) c q -> d h c q", d=DH)
                        for r, part in enumerate(parts):
                            sp.dma_start(dst[r * DH:(r + 1) * DH, heads, :], src[:, :, part, :]).then_inc(s[landed], 16)

            def load_later(g):
                if g == 0:
                    load(xs[:, NB:, :], xv[:, NB:, :], "x_rest_in")
                elif g == 2:
                    load(w13[:], w13T.rearrange("(k p) n -> p k n", p=P), "ffn_in")
                elif g == 1:
                    load(b13[:], b13T, "ffn_in")
                    load(a13[:], a13T.rearrange("(k p) n -> p k n", p=P), "ffn_in")
                else:
                    sp.wait_ge(s["zero_done"], 3)
                    load(w2[:, 0:NF, :], w2T[0:NF * P].rearrange("(f p) n -> p f n", p=P), "ffn_in")
                    load(w2[0:FT, NF, :], w2T[NF * P:F], "ffn_in")
                    load(a2[:, 0:NF, :], a2T[0:NF * P].rearrange("(f p) n -> p f n", p=P), "ffn_in")
                    load(a2[0:FT, NF, :], a2T[NF * P:F], "ffn_in")
                    load(b2[:], b2T, "ffn_in")

            def run(ba, bf):
                for _, kind, n in merged("sp", ba is not None, bf is not None):
                    if kind == "lse":
                        n = n[1]
                        wait(sp, "lse_evac", ba, n + 1)
                        for i in range(3):
                            sp.dma_start(QA[R_NORM + i:R_NORM + i + 1, n * G:(n + 1) * G, :],
                                         lse_t[i * G * NB:(i + 1) * G * NB, :]).then_inc(s["lse_landed"], 16)
                        if bf is None:
                            load_later(n)
                    elif kind == "result":
                        for i in (2 * n, 2 * n + 1):
                            wait(sp, "o_ready", bf, i + 1)
                            sp.dma_start(out[bf, i * P:(i + 1) * P, :], xs[:, bf * NB + i, :]).then_inc(s["store_done"], 16)

            regroup(0)
            run(0, None)
            with sp.Fori(0, B - 1) as b:
                regroup(b + 1)
                run(b + 1, b)
            run(None, B - 1)
            sp.wait_ge(s["store_done"], B * per["store_done"])

        @block.gpsimd
        def _(pool):
            def load(dst, src, name):
                pool.dma_start(dst, src).then_inc(s[name], 16)

            wmod_v = wmod.rearrange("(k p) n -> p k n", p=P)
            load(wmod_s[:, :, 0:2 * D], wmod_v[:, :, 0:2 * D], "wmod_in")
            nc.gpsimd.memset(V[:], 0.0).then_inc(s["zero_done"], 1)
            nc.gpsimd.memset(w2[:], 0.0).then_inc(s["zero_done"], 1)
            nc.gpsimd.memset(a2[:], 0.0).then_inc(s["zero_done"], 1)
            nc.gpsimd.memset(floor_c[:], PROB_FLOOR).then_inc(s["zero_done"], 1)
            nc.gpsimd.memset(half_c[:], 0.5).then_inc(s["zero_done"], 1)
            pool.wait_ge(s["zero_done"], 3)
            load(wmod_s[:, :, 2 * D:], wmod_v[:, :, 2 * D:], "wmod_rest_in")
            wov = woT.rearrange("(g2 o c d) n -> o c d g2 n", g2=NG // 2, o=2, c=G)
            for odd in range(2):
                for c in range(G):
                    load(wo[32 * c + odd * DH:32 * c + (odd + 1) * DH, :, :], wov[odd, c], "out_w_in")
            def front(b):
                wait(pool, "v_ready", b, 2 * NB)
                nc.gpsimd.tensor_tensor(Vsuf[:, 1], V[:, 2], V[:, 3], ALU.add).then_inc(s["vsuf_mid"], 1)
                wait(pool, "vsuf_mid", b, 1)
                nc.gpsimd.tensor_tensor(Vsuf[:, 0], V[:, 1], Vsuf[:, 1], ALU.add).then_inc(s["vsuf_ready"], 1)

            def bias_of_y(b):
                nc.gpsimd.tensor_tensor(gbias, gates[:, b, 0, :], b_o[:], ALU.mult).then_inc(s["gbias_ready"], 1)
                wait(pool, "gbias_ready", b, 1)
                for i in range(NB):
                    nc.gpsimd.tensor_tensor(xs[:, b * NB + i, :], xs[:, b * NB + i, :], gbias, ALU.add).then_inc(s["x_biased"], 1)

            def routing(b):
                wait(pool, "pickT_ready", b, 2)
                nc.gpsimd.tensor_tensor(pickw[:, 2, :], pickT[:, 1, :], pickT[:, 0, :], ALU.subtract).then_inc(s["pickd_ready"], 1)
                wait(pool, "pickT_ready", b, 4)
                for k in range(2):
                    nc.gpsimd.tensor_tensor(pickw[:, k, :], pickT[:, k, :], pickT[:, 2 + k, :], ALU.mult).then_inc(s["pickw_ready"], 1)

            def run(ba, bf):
                for _, kind, n in merged("pool", ba is not None, bf is not None):
                    if kind == "norm":
                        z = zsum[:, G * n:G * (n + 1), :].rearrange("p h i -> p (h i)")
                        wait_apart(pool, "p1_done", ba, 2 * UNITS * (n + 1))
                        nc.gpsimd.tensor_copy(zbits[:], z.bitcast(U32)).then_inc(s["zbits_ready"], 1)
                        wait_apart(pool, "zbits_ready", ba, n + 1)
                        nc.gpsimd.tensor_scalar(logz[:], zbits[:], LN_SLOPE, -LN_AT_ZERO, ALU.mult, ALU.add).then_inc(s["log_ready"], 1)
                        wait_apart(pool, "log_ready", ba, n + 1)
                        nc.gpsimd.tensor_tensor(lse[:], shift[:, G * n:G * (n + 1), :].rearrange("p h i -> p (h i)"), logz[:],
                                                ALU.subtract).then_inc(s["lse_first"], 1)
                    elif kind == "lse":
                        n = n[1]
                        z = zsum[:, G * n:G * (n + 1), :].rearrange("p h i -> p (h i)")
                        wait_apart(pool, "zinv_ready", ba, n + 1)
                        nc.gpsimd.tensor_tensor(za[:], z, zinv[:], ALU.mult).then_inc(s["log_poly"], 1)
                        wait_apart(pool, "log_poly", ba, 8 * n + 1)
                        nc.gpsimd.tensor_scalar(ze[:], za[:], 1.0, None, ALU.subtract).then_inc(s["log_poly"], 1)
                        wait_apart(pool, "log_poly", ba, 8 * n + 2)
                        nc.gpsimd.tensor_scalar(za[:], ze[:], -1 / 4, 1 / 3, ALU.mult, ALU.add).then_inc(s["log_poly"], 1)
                        wait_apart(pool, "log_poly", ba, 8 * n + 3)
                        nc.gpsimd.tensor_tensor(za[:], za[:], ze[:], ALU.mult).then_inc(s["log_poly"], 1)
                        wait_apart(pool, "log_poly", ba, 8 * n + 4)
                        nc.gpsimd.tensor_scalar(za[:], za[:], -1 / 2, None, ALU.add).then_inc(s["log_poly"], 1)
                        wait_apart(pool, "log_poly", ba, 8 * n + 5)
                        nc.gpsimd.tensor_tensor(za[:], za[:], ze[:], ALU.mult).then_inc(s["log_poly"], 1)
                        wait_apart(pool, "log_poly", ba, 8 * n + 6)
                        nc.gpsimd.tensor_scalar(za[:], za[:], 1.0, None, ALU.add).then_inc(s["log_poly"], 1)
                        wait_apart(pool, "log_poly", ba, 8 * n + 7)
                        nc.gpsimd.tensor_tensor(za[:], za[:], ze[:], ALU.mult).then_inc(s["log_poly"], 1)
                        wait_apart(pool, "log_poly", ba, 8 * n + 8)
                        nc.gpsimd.tensor_tensor(lse[:], lse[:], za[:], ALU.subtract).then_inc(s["lse_ready"], 1)
                        wait_apart(pool, "lse_ready", ba, n + 1)
                        nc.gpsimd.tensor_copy(lse_p[:, 0, :], lse[:]).then_inc(s["lse_hi"], 1)
                        wait_apart(pool, "lse_hi", ba, n + 1)
                        nc.gpsimd.tensor_tensor(lse_r[:], lse[:], lse_p[:, 0, :], ALU.subtract).then_inc(s["lse_res"], 1)
                        wait_apart(pool, "lse_res", ba, n + 1)
                        nc.gpsimd.tensor_copy(lse_p[:, 1, :], lse_r[:]).then_inc(s["lse_mid"], 1)
                        wait_apart(pool, "lse_mid", ba, n + 1)
                        nc.gpsimd.tensor_tensor(lse_p[:, 2, :], lse_r[:], lse_p[:, 1, :], ALU.subtract).then_inc(s["lse_parts"], 1)
                    elif kind == "first":
                        f, cols, _, turn, m = of_step(n)
                        wait(pool, "fa_act", bf, n + 1)
                        if n >= 1:
                            wait(pool, "gsum_ready", bf, n)
                        nc.gpsimd.tensor_tensor(gw[0:m, 0, :], act1[0:m, turn, :], pickT[0:m, 2, cols], ALU.mult).then_inc(s["gw_ready"], 1)
                    elif kind == "second":
                        f, cols, _, turn, m = of_step(n)
                        wait(pool, "fb_act", bf, n + 1)
                        nc.gpsimd.tensor_tensor(gw[0:m, 1, :], act2[0:m, turn, :], pickT[0:m, 3, cols], ALU.mult).then_inc(s["gw_ready"], 1)
                        wait(pool, "gw_ready", bf, 2 * n + 2)
                        nc.gpsimd.tensor_tensor(gsum[0:m, turn, :], gw[0:m, 0, :], gw[0:m, 1, :], ALU.add).then_inc(s["gsum_ready"], 1)

            front(0)
            run(0, None)
            pool.wait_ge(s["gates_ready"], B)
            bias_of_y(0)
            with pool.Fori(0, B - 1) as b:
                front(b + 1)
                wait(pool, "h2T_ps", b, KT)
                bias_of_y(b + 1)
                routing(b)
                run(b + 1, b)
            routing(B - 1)
            run(None, B - 1)

        @block.scalar
        def _(act):
            def seed(tag, b):
                wait(act, f"{tag}_log", b, 1)
                nc.scalar.activation(rstd0[:], logv[:], ACT.Exp, scale=-0.5).then_inc(s[f"{tag}_seed"], 1)

            def modulate(b, n, dst, bank):
                wait(act, f"mod{n}_now", b, 1)
                for k in range(KT):
                    wait(act, f"h{n}T_ps", b, k + 1)
                    nc.scalar.activation(dst[:, k, :], ps[:, bank + k, :], ACT.Identity, scale=modc[:, n - 1, 1, k:k + 1],
                                         bias=modc[:, n - 1, 0, k:k + 1]).then_inc(s[f"h{n}T_ready"], 1)

            def evacuate_qk(b, n, t):
                wait(act, "qk_ps", b, n + 1)
                scale = SCALE if t < KT else 1.0
                nc.scalar.activation(qk_p[:, t, 0, :], ps[:, (n + 2) % 4, :], ACT.Identity, bias=b_qk[:, t:t + 1],
                                     scale=scale).then_inc(s["qk_hi"], 1)
                if n >= 2:
                    wait(act, "qk_res", b, n - 1)
                nc.scalar.activation(qk_f[:, n % 2, :], ps[:, (n + 2) % 4, :], ACT.Identity, bias=b_qk[:, t:t + 1],
                                     scale=scale).then_inc(s["qk_evac"], 1)

            def routing(b):
                wait(act, "rdiff_ready", b, 1)
                nc.scalar.activation(rexp[:], rdiff[:], ACT.Exp).then_inc(s["rexp_ready"], 1)
                for k in range(3):
                    bank = (5, 3, 5)[k]
                    wait(act, "pick_ps", b, k + 1)
                    nc.scalar.copy(pickT[:, k, :], ps[:, bank, :]).then_inc(s["pickT_ready"], 1)
                nc.scalar.activation(pickT[:, 3, :], ps[:, 5, :], ACT.Identity, scale=-1.0, bias=half_c[:]).then_inc(s["pickT_ready"], 1)

            def run(ba, bf, more=False):
                banks = ring(bf is not None)
                for _, kind, n in merged("act", ba is not None, bf is not None, more):
                    if kind == "p1":
                        at, i, parts = n
                        wait(act, "p1_max", ba, i + 1)
                        for h, blk, c in parts:
                            scores = ps[:, banks[at % len(banks)], c:c + WIDTH1[blk]]
                            last = nc.scalar.activation(scores, scores, ACT.Exp, scale=-1.0, bias=shift[:, h, blk:blk + 1],
                                                        accum_out=zsum[:, h, blk:blk + 1])
                        last.then_inc(s["p1_done"], 1)
                    elif kind == "next":
                        modulate(ba + 1, 1, hT, 0)
                    elif kind == "gates":
                        act.wait_ge(s["gate_wide"], n + 1)
                        nc.scalar.copy(gates[:, n].rearrange("p a d -> p (a d)"), ps[:, 6 + n % 2, :]).then_inc(s["gates_ready"], 1)
                    elif kind == "statistics":
                        seed("ln1", n)
                    elif kind == "norm":
                        wait(act, "log_ready", ba, n + 1)
                        nc.scalar.activation(zinv[:], logz[:], ACT.Exp, scale=-1.0).then_inc(s["zinv_ready"], 1)
                    elif kind == "lse":
                        at, n, _ = n
                        wait(act, "lse_ps", ba, n + 1)
                        if n >= 1:
                            wait(act, "lse_landed", ba, 48 * n)
                        nc.scalar.copy(lse_t[:], ps[:, banks[at % len(banks)], :].bitcast(BF16)[0:3 * G * NB, 0:P]).then_inc(s["lse_evac"], 1)
                    elif kind == "p2":
                        at, i, parts = n
                        p, u = i // UNITS, i % UNITS
                        slot = 2 * p % NPROB
                        wait(act, "p2_ps", ba, i + 1)
                        if 2 * p >= NPROB:
                            wait(act, "pv_ps", ba, (2 * p - NPROB) // G + 1)
                        if u:
                            v = u - 1
                            nc.scalar.activation(prob[:, slot + v // 2, (v % 2) * 512:(v % 2 + 1) * 512], ps[:, banks[at % len(banks)], :],
                                                 ACT.Exp).then_inc(s["p2_exp"], 1)
                        else:
                            nc.scalar.activation(prob[:, slot:slot + 2, 1024:1280], ps[:, banks[at % len(banks)], :].rearrange("p (h n) -> p h n", h=2),
                                                 ACT.Exp).then_inc(s["p2_exp"], 1)
                    elif kind == "pv" and n % 2:
                        wait(act, "pv_ps", ba, n + 1)
                        nc.scalar.copy(att[:, n // 2, :], ps[:, ATT_BANK, :]).then_inc(s["att_ready"], 1)
                    elif kind in ("first", "second"):
                        f, cols, bank, turn, m = of_step(n)
                        slot, x_ = (0, "fa") if kind == "first" else (1, "fb")
                        wait(act, x_ + "_ps", bf, n + 1)
                        if n >= 1:
                            wait(act, x_ + "_act", bf, n)
                        nc.scalar.activation(sil[0:m, slot, :], ps[0:m, bank, 0:HS], ACT.Tanh, scale=0.5).then_inc(s[x_ + "_tanh"], 1)

            act.wait_ge(s["c_in"], 16)
            nc.scalar.activation(c_silu[:], c_t[:], ACT.Silu).then_inc(s["cs_ready"], 1)
            seed("ln1", 0)
            modulate(0, 1, hT, 0)
            act.wait_ge(s["bq_scaled"], 1)
            for n, t in enumerate(QK_ORDER):
                evacuate_qk(0, n, t)
            def body(b, more):
                seed("ln2", b)
                for n, t in enumerate(QK_ORDER):
                    evacuate_qk(b + 1, n, t)
                modulate(b, 2, h2T, FFN_BANK)
                routing(b)
                run(b + 1, b, more)

            run(0, None, True)
            with act.Fori(0, B - 2) as b:
                body(b, True)
            body(B - 2, False)
            seed("ln2", B - 1)
            modulate(B - 1, 2, h2T, FFN_BANK)
            routing(B - 1)
            run(None, B - 1)

        @block.vector
        def _(dve):
            def row_stats(tag, b, mv, rstd):
                v, bits, lg, r0, a, e = [t_[:] for t_ in (veps, vbits, logv, rstd0, ra, re)]
                for i in range(NB):
                    nc.vector.bn_stats(stats[:, i, :], xs[:, b * NB + i, :]).then_inc(s[f"{tag}_stat"], 1)
                for i in range(NB):
                    wait_apart(dve, f"{tag}_stat", b, i + 1)
                    nc.vector.bn_aggr(mv[:, i, :], stats[:, i, :]).then_inc(s[f"{tag}_aggr"], 1)
                wait(dve, f"{tag}_aggr", b, NB)
                nc.vector.tensor_scalar(v, mv[:, :, 1], LN_EPS, None, ALU.add).then_inc(s[f"{tag}_veps"], 1)
                wait(dve, f"{tag}_veps", b, 1)
                nc.vector.tensor_copy(bits, v.bitcast(U32)).then_inc(s[f"{tag}_bits"], 1)
                wait(dve, f"{tag}_bits", b, 1)
                nc.vector.tensor_scalar(lg, bits, LN_SLOPE, -LN_AT_ZERO, ALU.mult, ALU.add).then_inc(s[f"{tag}_log"], 1)
                poly = f"{tag}_poly"
                wait(dve, f"{tag}_seed", b, 1)
                nc.vector.tensor_tensor(a, r0, r0, ALU.mult).then_inc(s[poly], 1)
                wait(dve, poly, b, 1)
                nc.vector.tensor_tensor(a, a, v, ALU.mult).then_inc(s[poly], 1)
                wait(dve, poly, b, 2)
                nc.vector.tensor_scalar(e, a, -1.0, 1.0, ALU.mult, ALU.add).then_inc(s[poly], 1)
                wait(dve, poly, b, 3)
                nc.vector.tensor_scalar(a, e, 35 / 128, 5 / 16, ALU.mult, ALU.add).then_inc(s[poly], 1)
                wait(dve, poly, b, 4)
                nc.vector.tensor_tensor(a, a, e, ALU.mult).then_inc(s[poly], 1)
                wait(dve, poly, b, 5)
                nc.vector.scalar_tensor_tensor(out=a, in0=a, scalar=3 / 8, in1=e, op0=ALU.add, op1=ALU.mult).then_inc(s[poly], 1)
                wait(dve, poly, b, 6)
                nc.vector.scalar_tensor_tensor(out=a, in0=a, scalar=1 / 2, in1=e, op0=ALU.add, op1=ALU.mult).then_inc(s[poly], 1)
                wait(dve, poly, b, 7)
                nc.vector.scalar_tensor_tensor(out=rstd, in0=a, scalar=1.0, in1=r0, op0=ALU.add, op1=ALU.mult).then_inc(s[poly], 1)
                wait(dve, poly, b, 8)

            def normalise(b, n, xhat, mv, rstd):
                for i in range(NB):
                    nc.vector.tensor_scalar(xhat[:, i, :], xs[:, b * NB + i, :], mv[:, i, 0:1], rstd[:, i:i + 1],
                                            ALU.subtract, ALU.mult).then_inc(s[f"ln{n}_xhat"], 1)

            def mod_of(b, n):
                nc.vector.tensor_copy(modc[:, n - 1].rearrange("p a k -> p (a k)"),
                                      mod_t[:, 2 * n - 2:2 * n].rearrange("p a k b -> p (a k) b")[:, :, b]).then_inc(s[f"mod{n}_now"], 1)

            def split_qk(b, n, t):
                wait(dve, "qk_evac", b, n + 1)
                wait(dve, "qk_hi", b, n + 1)
                if n:
                    wait(dve, "qk_parts", b, n)
                nc.vector.tensor_tensor(qk_r, qk_f[:, n % 2, :], qk_p[:, t, 0, :], ALU.subtract).then_inc(s["qk_res"], 1)
                wait(dve, "qk_res", b, n + 1)
                nc.vector.tensor_copy(qk_p[:, t, 1, :], qk_r).then_inc(s["qk_mid"], 1)
                wait(dve, "qk_mid", b, n + 1)
                nc.vector.tensor_tensor(qk_p[:, t, 2, :], qk_r, qk_p[:, t, 1, :], ALU.subtract).then_inc(s["qk_parts"], 1)

            def evacuate_v(b):
                for i in range(NB):
                    wait(dve, "v_ps", b, i // 2 * 2 + 2)
                    dst = V[:, i].rearrange("p (g2 o c) d -> p g2 o c d", g2=NG // 2, o=2)
                    src = ps[:, 2 + i // 2, (i % 2) * D:(i % 2 + 1) * D].rearrange("p (g2 o c d) -> p g2 o c d", g2=NG // 2, o=2, c=G)
                    bias = b_v[:].rearrange("p (g2 o c d) -> p g2 o c d", g2=NG // 2, o=2, c=G)
                    for odd in range(2):
                        nc.vector.tensor_tensor(dst[:, :, odd, :, odd * DH:(odd + 1) * DH], src[:, :, odd], bias[:, :, odd],
                                                ALU.add).then_inc(s["v_ready"], 1)

            def routing(b):
                wait(dve, "logit_ps", b, 1)
                nc.vector.tensor_copy(logit[:].rearrange("p i e -> p (i e)"), ps[:, 5, 0:NB * E]).then_inc(s["logit_ready"], 1)
                wait_apart(dve, "logit_ready", b, 1)
                for i in range(NB):
                    nc.vector.max(top[:, i, :], logit[:, i, :]).then_inc(s["top_ready"], 1)
                for i in range(NB):
                    wait_apart(dve, "top_ready", b, i + 1)
                    nc.vector.max_index(top_i[:, i, :], top[:, i, :], logit[:, i, :]).then_inc(s["topi_ready"], 1)
                nc.vector.tensor_tensor(rdiff[:], top[:, :, 1], top[:, :, 0], ALU.subtract).then_inc(s["rdiff_ready"], 1)
                wait(dve, "topi_ready", b, NB)
                nc.vector.tensor_copy(top_f[:], top_i[:, :, 0:2]).then_inc(s["topf_ready"], 1)
                wait(dve, "topf_ready", b, 1)
                for k in range(2):
                    for i in range(NB):
                        last = nc.vector.tensor_scalar(pick[:, k, i, :], ecol, top_f[:, i, k:k + 1], LORA_SCALE, ALU.is_equal, ALU.mult)
                    last.then_inc(s["pick_ready"], 1)
                wait(dve, "rexp_ready", b, 1)
                nc.vector.tensor_scalar(rsum[:], rexp[:], 1.0, 2.0, ALU.add, ALU.mult).then_inc(s["rsum_ready"], 1)
                wait(dve, "rsum_ready", b, 1)
                nc.vector.reciprocal(rw[:], rsum[:]).then_inc(s["rw_ready"], 1)
                wait(dve, "rw_ready", b, 1)
                for i in range(NB):
                    last = nc.vector.tensor_scalar(pick[:, 2, i, :], ecol, 0.0, rw[:, i:i + 1], ALU.mult, ALU.add)
                last.then_inc(s["pick_ready"], 1)
                wait(dve, "u_ps", b, 2)
                wait(dve, "pickT_ready", b, 1)
                for k in range(2):
                    nc.vector.tensor_tensor(um[:, k, :], ps[:, 6 + k, :], pickT[:, 0, :], ALU.mult).then_inc(s["um_ready"], 1)
                wait(dve, "pickd_ready", b, 1)
                for k in range(2):
                    nc.vector.tensor_tensor(um[:, 2 + k, :], ps[:, 6 + k, :], pickw[:, 2, :], ALU.mult).then_inc(s["um_ready"], 1)

            def run(ba, bf, more=False):
                banks = ring(bf is not None)
                results, projected = 0, False
                for _, kind, n in merged("dve", ba is not None, bf is not None, more):
                    if kind == "p1":
                        at, i, parts = n
                        wait_apart(dve, "p1_ps", ba, i + 1)
                        for h, blk, c in parts:
                            scores = ps[:, banks[at % len(banks)], c:c + WIDTH1[blk]]
                            last = nc.vector.tensor_tensor_reduce(out=scores, in0=scores, in1=qmask[:, S - WIDTH1[blk]:S], scale=-1.0,
                                                                  scalar=3.3e38, op0=ALU.add, op1=ALU.min, accum_out=shift[:, h, blk:blk + 1])
                        last.then_inc(s["p1_max"], 1)
                    elif kind == "floor":
                        slot = n % NPROB
                        wait(dve, "p2_exp", ba, UNITS * (n // 2) + 3 + 2 * (n % 2))
                        nc.vector.tensor_scalar(prob[:, slot, :], prob[:, slot, :], PROB_FLOOR, None, ALU.max).then_inc(s["p2_ready"], 1)
                    elif kind == "next":
                        wait(dve, "x_biased", ba, NB)
                        nc.vector.tensor_copy(mv_now[:], mv1[:, bass.ds((ba + 1) * NB, NB), 0:1]).then_inc(s["ln1_now"], 1)
                        nc.vector.tensor_copy(rstd_now[:], rstd1[:, bass.ds((ba + 1) * NB, NB)]).then_inc(s["ln1_now"], 1)
                        mod_of(ba + 1, 1)
                        wait(dve, "ln1_now", ba, 2)
                        normalise(ba + 1, 1, xhat, mv_now, rstd_now)
                    elif kind == "statistics":
                        dve.wait_ge(s["x_rest_in"], 16)
                        row_stats("ln1", n, mv1[:, n * NB:(n + 1) * NB], rstd1[:, n * NB:(n + 1) * NB])
                    elif kind == "y":
                        wait(dve, "x_biased", ba, NB)
                        if results:
                            wait(dve, "o_ready", bf, 2 * results)
                        projected = True
                        for t in range(NB // 2):
                            wait(dve, "y_ps", ba, 2 * t + 2)
                            if t:
                                wait(dve, "x1_ready", ba, 2 * t)
                            for i in (2 * t, 2 * t + 1):
                                nc.vector.tensor_tensor(ysb[:, i % 2, :], ps[:, 2 + t, (i % 2) * D:(i % 2 + 1) * D], gates[:, ba, 0, :],
                                                        ALU.mult).then_inc(s["y_gated"], 1)
                            for i in (2 * t, 2 * t + 1):
                                wait(dve, "y_gated", ba, i + 1)
                                nc.vector.tensor_tensor(xs[:, ba * NB + i, :], xs[:, ba * NB + i, :], ysb[:, i % 2, :],
                                                        ALU.add).then_inc(s["x1_ready"], 1)
                    elif kind in ("first", "second"):
                        f, cols, bank, turn, m = of_step(n)
                        slot, x_, dst = (0, "fa", act1) if kind == "first" else (1, "fb", act2)
                        m0 = 0 if f < NF else FT
                        wait(dve, x_ + "_tanh", bf, n + 1)
                        nc.vector.scalar_tensor_tensor(out=sil[m0:m0 + m, slot, :], in0=sil[0:m, slot, :], scalar=1.0, in1=ps[0:m, bank, 0:HS],
                                                       op0=ALU.add, op1=ALU.mult).then_inc(s[x_ + "_gate"], 1)
                        wait(dve, x_ + "_gate", bf, n + 1)
                        if n >= 2:
                            wait(dve, "down_ps", bf, n - 1)
                        h3 = ps[:, bank, HS:2 * HS] if f < NF else ps[FT:2 * FT, bank, 0:HS]
                        nc.vector.tensor_tensor(dst[0:m, turn, :], h3, sil[m0:m0 + m, slot, :], ALU.mult).then_inc(s[x_ + "_act"], 1)
                    elif kind == "weigh":
                        cols = slice(n * HS, (n + 1) * HS)
                        wait(dve, "down_ps", bf, NFT * (n + 1))
                        wait(dve, "pickw_ready", bf, 2)
                        if n:
                            wait(dve, "o_ps", bf, 2)
                        nc.vector.tensor_tensor(tm[:, 0, :], ps[:, T_BANK, 0:HS], pickw[:, 0, cols], ALU.mult).then_inc(s["tm_1"], 1)
                        nc.vector.tensor_tensor(tm[:, 1, :], ps[:, T_BANK, HS:2 * HS], pickw[:, 1, cols], ALU.mult).then_inc(s["tm_2"], 1)
                        wait(dve, "tm_2", bf, n + 1)
                        nc.vector.tensor_tensor(tm[:, 0, :], tm[:, 0, :], tm[:, 1, :], ALU.add).then_inc(s["tm_ready"], 1)
                    elif kind == "result":
                        wait(dve, "o_ps", bf, 2 * n + 2)
                        if n:
                            wait(dve, "o_ready", bf, 2)
                        if projected:
                            wait(dve, "x1_ready", ba, NB)
                        results += 1
                        for i in (2 * n, 2 * n + 1):
                            nc.vector.tensor_tensor(osb[:, i % 2, :], ps[:, OUT_BANK, (i % 2) * D:(i % 2 + 1) * D], gates[:, bf, 1, :],
                                                    ALU.mult).then_inc(s["o_gated"], 1)
                        for i in (2 * n, 2 * n + 1):
                            wait(dve, "o_gated", bf, i + 1)
                            nc.vector.tensor_tensor(xs[:, bf * NB + i, :], xs[:, bf * NB + i, :], osb[:, i % 2, :],
                                                    ALU.add).then_inc(s["o_ready"], 1)

            dve.wait_ge(s["x_in"], 16)
            row_stats("ln1", 0, mv1[:, 0:NB], rstd1[:, 0:NB])
            normalise(0, 1, xhat, mv1, rstd1)
            mods = ps[:, 4, 0:4 * KT * B].rearrange("p (a k b) -> p a k b", a=4, k=KT)
            for a in range(2):
                dve.wait_ge(s["mod_ps"], 1)
                nc.vector.tensor_scalar(mod_t[:, a], mods[:, a], float(a % 2), None, ALU.add).then_inc(s["modt_ready"], 1)
            dve.wait_ge(s["modt_ready"], 2)
            mod_of(0, 1)
            dve.wait_ge(s["small_in"], 80)
            nc.vector.tensor_copy(slope_p[:, 0:1], slope[:]).then_inc(s["sl_1"], 1)
            dve.wait_ge(s["sl_1"], 1)
            nc.vector.tensor_tensor(slope_r[:, 0:1], slope[:], slope_p[:, 0:1], ALU.subtract).then_inc(s["sl_2"], 1)
            dve.wait_ge(s["sl_2"], 1)
            nc.vector.tensor_copy(slope_p[:, 1:2], slope_r[:, 0:1]).then_inc(s["sl_3"], 1)
            dve.wait_ge(s["sl_3"], 1)
            nc.vector.tensor_tensor(slope_p[:, 2:3], slope_r[:, 0:1], slope_p[:, 1:2], ALU.subtract).then_inc(s["sl_4"], 1)
            dve.wait_ge(s["sl_4"], 1)
            dve.wait_ge(s["const_in"], 16)
            for i in range(3):
                for sign in (1.0, -1.0):
                    nc.vector.tensor_scalar(slope_w[:, i if sign > 0 else 3 + i, :], slope_p[:, i:i + 1].to_broadcast([H, S]),
                                            sign, None, ALU.mult).then_inc(s["slope_wide"], 1)
            nc.vector.tensor_scalar(b_qk[:, 0:KT], b_qk[:, 0:KT], SCALE, None, ALU.mult).then_inc(s["bq_scaled"], 1)
            nc.vector.tensor_copy(ident_b[:], ident).then_inc(s["const_ready"], 1)
            nc.vector.tensor_copy(kmask_b[:], kmask).then_inc(s["const_ready"], 1)
            nc.vector.tensor_copy(select, const[0:B, 0:B].rearrange("p (b o) -> p b o", o=1).to_broadcast([B, B, P])).then_inc(s["select_ready"], 1)
            dve.wait_ge(s["zero_done"], 5)
            for n, t in enumerate(QK_ORDER):
                split_qk(0, n, t)
            evacuate_v(0)
            for a in (2, 3):
                dve.wait_ge(s["mod_ps"], 2)
                nc.vector.tensor_scalar(mod_t[:, a], mods[:, a], float(a % 2), None, ALU.add).then_inc(s["modt_ready"], 1)
            dve.wait_ge(s["gate_ps"], 1)
            g = ps[0:B, 5, :]
            nc.vector.tensor_scalar(g_abs, g, -1.0, None, ALU.mult).then_inc(s["gate_neg"], 1)
            dve.wait_ge(s["gate_neg"], 1)
            nc.vector.tensor_tensor(g_abs, g, g_abs, ALU.max).then_inc(s["gate_abs"], 1)
            nc.vector.tensor_scalar(g_sgn, g, 0.0, 2.0, ALU.is_ge, ALU.mult).then_inc(s["gate_sgn"], 1)
            dve.wait_ge(s["gate_sgn"], 1)
            nc.vector.tensor_scalar(g_abs, g_abs, GATE_FLOOR, None, ALU.max).then_inc(s["gate_floor"], 1)
            dve.wait_ge(s["gate_floor"], 1)
            nc.vector.scalar_tensor_tensor(out=g_all, in0=g_sgn, scalar=-1.0, in1=g_abs, op0=ALU.add, op1=ALU.mult).then_inc(s["gate_rows"], 1)
            dve.wait_ge(s["gate_rows"], 1)
            def body(b, more):
                wait_apart(dve, "x1_ready", b, NB)
                row_stats("ln2", b, mv2[:], rstd2[:])
                wait(dve, "h1T_ps", b + 1, KT)
                normalise(b, 2, xhat, mv2, rstd2)
                mod_of(b, 2)
                for n, t in enumerate(QK_ORDER):
                    split_qk(b + 1, n, t)
                evacuate_v(b + 1)
                routing(b)
                run(b + 1, b, more)

            run(0, None, True)
            with dve.Fori(0, B - 2) as b:
                body(b, True)
            body(B - 2, False)
            wait_apart(dve, "x1_ready", B - 1, NB)
            row_stats("ln2", B - 1, mv2[:], rstd2[:])
            normalise(B - 1, 2, xhat, mv2, rstd2)
            mod_of(B - 1, 2)
            routing(B - 1)
            run(None, B - 1)

        @block.tensor
        def _(pe):
            mm = nc.tensor.matmul

            def transposes(b, n, xhat, bank):
                for k in range(KT):
                    for i in range(NB):
                        wait(pe, f"ln{n}_xhat", b, i + 1)
                        last = nc.tensor.transpose(ps[:, bank + k, i * P:(i + 1) * P], xhat[:, i, k * P:(k + 1) * P], ident)
                    last.then_inc(s[f"h{n}T_ps"], 1)

            def front(b):
                wait(pe, "h1T_ready", b, KT)
                for n, t in enumerate(QK_ORDER):
                    for k in range(KT):
                        last = mm(ps[:, (n + 2) % 4, :], wqkv[:, k, t * P:(t + 1) * P], hT[:, k, :], start=k == 0, stop=k == KT - 1)
                    last.then_inc(s["qk_ps"], 1)

            def front_v(b):
                wait(pe, "qk_evac", b, 2)
                for i in range(NB):
                    for k in range(KT):
                        last = mm(ps[:, 2 + i // 2, (i % 2) * D:(i % 2 + 1) * D], hT[:, k, i * P:(i + 1) * P],
                                  wqkv[:, k, 2 * D:3 * D], start=k == 0, stop=k == KT - 1)
                    last.then_inc(s["v_ps"], 1)

            def targets(n):
                f, _, bank, _, _ = of_step(n)
                c0, _ = tile_cols(f)
                return [(ps[:, bank, 0:HS], c0), (ps[:, bank, HS:2 * HS], c0 + P)][:2 if f < NF else 1]

            def base(b, n, j):
                f, cols, bank, _, _ = of_step(n)
                if n == 1 and j == 0:
                    wait(pe, "pickT_ready", b, 4)
                if n >= 2 and j == 0:
                    wait(pe, "fb_act", b, n - 1)
                if j < len(targets(n)):
                    dst, c0 = targets(n)[j]
                    for k in range(KT):
                        mm(dst, w13[:, k, c0:c0 + P], h2T[:, k, cols], start=j == 0 and k == 0, stop=True, skip_group_check=True)

            def lora(b, n, slot):
                f, cols, bank, _, _ = of_step(n)
                if n == 0:
                    wait(pe, "um_ready", b, 2 + 2 * slot)
                if slot == 1:
                    wait(pe, "fa_act", b, n + 1)
                for j, (dst, c0) in enumerate(targets(n)):
                    if f < NF:
                        last = mm(dst, b13[:, c0:c0 + P], um[:, 2 * slot + j, cols], start=False, stop=True, skip_group_check=True)
                    else:
                        for q in range(2):
                            last = mm(dst[q * FT:(q + 1) * FT], b13[:, c0 + q * FT:c0 + (q + 1) * FT], um[:, 2 * slot + q, cols],
                                      start=False, stop=True, skip_group_check=True)
                last.then_inc(s["fb_ps" if slot else "fa_ps"], 1)

            def ffn_front(b):
                wait(pe, "h2T_ready", b, KT)
                for i in range(NB):
                    for k in range(KT):
                        last = mm(ps[:, 5, i * E:(i + 1) * E], h2T[:, k, i * P:(i + 1) * P], gate_w[:, k, :], start=k == 0, stop=k == KT - 1)
                last.then_inc(s["logit_ps"], 1)
                for t in range(2):
                    for k in range(KT):
                        last = mm(ps[:, 6 + t, :], a13[:, k, t * P:(t + 1) * P], h2T[:, k, :], start=k == 0, stop=k == KT - 1)
                    last.then_inc(s["u_ps"], 1)
                base(b, 0, 0)
                base(b, 0, 1)
                for k in range(3):
                    bank = (5, 3, 5)[k]
                    wait(pe, "pick_ready", b, k + 1)
                    if k == 2:
                        wait(pe, "pickT_ready", b, 1)
                    for i in range(NB):
                        last = nc.tensor.transpose(ps[:, bank, i * P:(i + 1) * P], pick[:, k, i, :], ident)
                    last.then_inc(s["pick_ps"], 1)

            def run(ba, bf, more=False):
                banks = ring(bf is not None)
                for _, kind, n in merged("pe", ba is not None, bf is not None, more):
                    if kind in ("p1", "p2", "lse"):
                        at, i, parts = n
                        if kind == "lse":
                            wait_apart(pe, "lse_parts", ba, i + 1)
                        if at == 0:
                            wait(pe, "rows_a_landed", ba, per["rows_a_landed"])
                            wait(pe, "v_ready", ba, 2 * NB)
                            wait(pe, "qk_evac", ba, NQK)
                        if at == place["p1", UNITS * PAIRS // 2]:
                            wait(pe, "rows_b_landed", ba, per["rows_b_landed"])
                        if at >= len(banks):
                            was, j, _ = units[at - len(banks)]
                            (wait_apart if kind == "lse" else wait)(pe, {"p1": "p1_done", "p2": "p2_exp", "lse": "lse_evac"}[was], ba, j + 1)
                    if kind == "p1":
                        for h, blk, c in parts:
                            last = mm(ps[:, banks[at % len(banks)], c:c + WIDTH1[blk]], QA[0:R_NORM, h, blk * P:(blk + 1) * P],
                                      KA[0:R_NORM, h, 0:WIDTH1[blk]], start=True, stop=True)
                        last.then_inc(s["p1_ps"], 1)
                    elif kind == "p2":
                        if i % (2 * UNITS) == 0:
                            wait(pe, "lse_landed", ba, 48 * (i // (2 * UNITS) + 1))
                        for h, blk, c in parts:
                            mm(ps[:, banks[at % len(banks)], c:c + P], ident_b[:], kmask_b[:], start=True, stop=True)
                            last = mm(ps[:, banks[at % len(banks)], c:c + WIDTH2[blk]], KA[0:R_ALL, h, blk * P:(blk + 1) * P], QA[0:R_ALL, h, blk * P:S],
                                      start=False, stop=True, skip_group_check=True)
                        last.then_inc(s["p2_ps"], 1)
                    elif kind == "next":
                        wait(pe, "p2_exp", ba, UNITS * PAIRS)
                        transposes(ba + 1, 1, xhat, 0)
                    elif kind == "gates":
                        if n >= 2:
                            pe.wait_ge(s["gates_ready"], n - 1)
                        mm(ps[:, 6 + n % 2, :], select[:, n, :], g_all, start=True, stop=True).then_inc(s["gate_wide"], 1)
                    elif kind == "lse":
                        nc.tensor.transpose(ps[:, banks[at % len(banks)], :].bitcast(BF16)[0:3 * G * NB, 0:P],
                                            lse_p[:].rearrange("p c n -> p (c n)"), ident_b[:]).then_inc(s["lse_ps"], 1)
                    elif kind == "pv":
                        n, part = n
                        if part == 0:
                            wait(pe, "p2_ready", ba, G * (n + 1))
                            if n == 0:
                                wait(pe, "vsuf_ready", ba, 1)
                            elif n == 2:
                                wait(pe, "att_ready", ba, 1)
                            for i in range(NB - 1):
                                for c in range(G):
                                    hh = G * n + c
                                    v = V[:, 3, hh, :] if i == 2 else Vsuf[:, i, hh, :]
                                    mm(ps[32 * c:32 * c + 32, ATT_BANK, i * P:(i + 1) * P], v, floor_c[:], start=i == 0 and n % 2 == 0, stop=True,
                                       skip_group_check=True)
                        j = NB - 1 - part
                        for c in range(G):
                            hh = G * n + c
                            last = mm(ps[32 * c:32 * c + 32, ATT_BANK, j * P:S], V[:, j, hh, :],
                                      prob[:, hh % NPROB, START2[j]:START2[j] + WIDTH2[j]], start=False, stop=True,
                                      skip_group_check=True)
                        if part == NB - 1:
                            last.then_inc(s["pv_ps"], 1)
                    elif kind == "y":
                        if bf is None:
                            pe.wait_ge(s["out_w_in"], 128)
                        wait(pe, "att_ready", ba, NG // 2)
                        wait(pe, "p2_exp", ba, UNITS * PAIRS)
                        for i in range(NB):
                            for g in range(NG // 2):
                                last = mm(ps[:, 2 + i // 2, (i % 2) * D:(i % 2 + 1) * D], att[:, g, i * P:(i + 1) * P], wo[:, g, :],
                                          start=g == 0, stop=g == NG // 2 - 1)
                            last.then_inc(s["y_ps"], 1)
                    elif kind == "base":
                        if n[0]:
                            base(bf, *n)
                    elif kind == "first":
                        lora(bf, n, 0)
                    elif kind == "second":
                        lora(bf, n, 1)
                    elif kind == "down_t":
                        f, cols, _, turn, _ = of_step(n)
                        wait(pe, "gsum_ready", bf, n + 1)
                        if n == NFT:
                            wait(pe, "tm_2", bf, 1)
                        mm(ps[:, T_BANK, 0:HS], a2[:, f, :], act1[:, turn, :], start=f == 0, stop=True, skip_group_check=True)
                        mm(ps[:, T_BANK, HS:2 * HS], a2[:, f, :], act2[:, turn, :], start=False, stop=True, skip_group_check=True)
                    elif kind == "down_o":
                        f, cols, _, turn, _ = of_step(n)
                        if n == NFT:
                            wait(pe, "o_gated", bf, 2)
                        for i in range(2):
                            last = mm(ps[:, OUT_BANK, i * D:(i + 1) * D], gsum[:, turn, i * P:(i + 1) * P], w2[:, f, :],
                                      start=f == 0 and i == 0, stop=True, skip_group_check=True)
                        last.then_inc(s["down_ps"], 1)
                    elif kind == "result":
                        wait(pe, "tm_ready", bf, n + 1)
                        for i in range(2):
                            mm(ps[:, OUT_BANK, i * D:(i + 1) * D], tm[:, 0, i * P:(i + 1) * P], b2[:], start=False, stop=True,
                               skip_group_check=True).then_inc(s["o_ps"], 1)

            pe.wait_ge(s["wmod_in"], 16)
            pe.wait_ge(s["cs_ready"], 1)
            def modulation(a, chunk):
                for t in range(KT):
                    for k in range(KT):
                        last = mm(ps[:, 4, (a * KT + t) * B:(a * KT + t + 1) * B], wmod_s[:, k, chunk * D + t * P:chunk * D + (t + 1) * P],
                                  c_silu[:, k, :], start=k == 0, stop=k == KT - 1)
                return last

            modulation(0, 0)
            modulation(1, 1).then_inc(s["mod_ps"], 1)
            pe.wait_ge(s["wqkv_in"], 16)
            pe.wait_ge(s["const_in"], 16)
            transposes(0, 1, xhat, 0)
            front(0)
            front_v(0)
            pe.wait_ge(s["wmod_rest_in"], 16)
            pe.wait_ge(s["modt_ready"], 2)
            modulation(2, 3)
            modulation(3, 4).then_inc(s["mod_ps"], 1)
            for n, chunk in enumerate((2, 5)):
                for k in range(KT):
                    last = mm(ps[0:B, 5, n * D:(n + 1) * D], c_silu[:, k, :], wmod_s[:, k, chunk * D:(chunk + 1) * D], start=k == 0, stop=k == KT - 1)
            last.then_inc(s["gate_ps"], 1)
            pe.wait_ge(s["rows_in"], 16 * 15)
            pe.wait_ge(s["select_ready"], 1)
            pe.wait_ge(s["const_ready"], 2)
            pe.wait_ge(s["modt_ready"], 4)
            pe.wait_ge(s["gate_rows"], 1)
            run(0, None, True)
            pe.wait_ge(s["ffn_in"], 128)
            pe.wait_ge(s["small_in"], 80)
            def body(b, more):
                wait(pe, "y_gated", b, NB)
                front(b + 1)
                transposes(b, 2, xhat, FFN_BANK)
                front_v(b + 1)
                ffn_front(b)
                run(b + 1, b, more)

            with pe.Fori(0, B - 2) as b:
                body(b, True)
            body(B - 2, False)
            wait(pe, "x1_ready", B - 1, NB)
            transposes(B - 1, 2, xhat, FFN_BANK)
            ffn_front(B - 1)
            run(None, B - 1)


_OUT = (4, 512, 256)


def kernel(L0_attn_qkv, L0_attn_in_proj, L0_attn_in_proj_bias, L0_attn_out_w, L0_attn_out_b, L0_attn_alibi_slopes, L0_ffn_gate_w,
           L0_ffn_w1, L0_ffn_w3, L0_ffn_w2, L0_ffn_a1, L0_ffn_b1, L0_ffn_a3, L0_ffn_b3, L0_ffn_a2, L0_ffn_b2, L0_c, L0_wmod):
    import numpy as np
    import ml_dtypes
    import concourse.bacc as bacc
    from concourse.bass_utils import run_bass_kernel_spmd

    a = {k: np.asarray(v) for k, v in dict(
        x=L0_attn_qkv, in_proj=L0_attn_in_proj, bqkv=L0_attn_in_proj_bias, out_w=L0_attn_out_w, bo=L0_attn_out_b,
        slopes=L0_attn_alibi_slopes, gate=L0_ffn_gate_w, w1=L0_ffn_w1, w3=L0_ffn_w3, w2=L0_ffn_w2, a1=L0_ffn_a1, b1=L0_ffn_b1,
        a3=L0_ffn_a3, b3=L0_ffn_b3, a2=L0_ffn_a2, b2=L0_ffn_b2, c=L0_c, wmod=L0_wmod).items()}
    E, R, D = a["a1"].shape
    F = a["w1"].shape[0]

    def pair(u, v):
        cuts = list(range(0, F, 128))
        return np.concatenate([m[:, n:n + 128] for n in cuts for m in (u, v)], axis=1)

    def ranks(w):
        return w.transpose(0, 2, 1).reshape(E * R, w.shape[1])

    n = np.arange(128)
    consts = np.zeros((128, 896), np.float32)
    consts[:, 0:128] = np.eye(128)
    consts[:, 128 + 384:640] = np.where(n[None, :] > n[:, None], MASKED, 0.0)
    consts[:, 640:768] = np.where(n[:, None] > n[None, :], MASKED, 0.0)
    consts[:, 768:896] = n[None, :] // R
    pos = np.ones((2, 1, 16, 512), np.float32)
    pos[0] = np.arange(512) - 256
    arrays = dict(
        x=a["x"], wqkvT=a["in_proj"].T, bqk=a["bqkv"][:2 * D].reshape(-1, 128).T, bv=a["bqkv"][2 * D:], woT=a["out_w"].T, bo=a["bo"], slopes=a["slopes"], gateT=a["gate"].T,
        w13T=pair(a["w1"].T, a["w3"].T), w2T=a["w2"].T, a13T=np.concatenate([a["a1"].reshape(E * R, D).T, a["a3"].reshape(E * R, D).T], axis=1),
        b13T=pair(ranks(a["b1"]), ranks(a["b3"])), a2T=a["a2"].reshape(E * R, F).T, b2T=ranks(a["b2"]), cT=a["c"].T, wmod=a["wmod"],
        consts=consts, pos_rows=pos.astype(ml_dtypes.bfloat16))
    nc = bacc.Bacc("TRN2", target_bir_lowering=False, num_devices=1)
    feed, args = {}, []
    for name, v in arrays.items():
        v = np.ascontiguousarray(v)
        feed[f"in_{name}"] = v
        args.append(nc.dram_tensor(f"in_{name}", v.shape, mybir.dt.from_np(v.dtype), kind="ExternalInput").ap())
    args.append(nc.dram_tensor("result", _OUT, F32, kind="ExternalOutput").ap())
    adaln_block(nc, *args)
    return run_bass_kernel_spmd(nc, [feed], core_ids=[0]).results[0]["result"]
```
